# Optimizing a Trainium2 kernel written in Bass

```python
import numpy as np
import jax
import jax.numpy as jnp

def _softmax(x, axis=-1):
    return jax.nn.softmax(x, axis=axis)

def _gelu(x):
    return jax.nn.gelu(x, approximate=True)

def _silu(x):
    return jax.nn.silu(x)

def _sigmoid(x):
    return jax.nn.sigmoid(x)

def _layernorm(x, axis=-1, eps=1e-05):
    m = jnp.mean(x, axis=axis, keepdims=True)
    v = jnp.var(x, axis=axis, keepdims=True)
    return (x - m) / jnp.sqrt(v + eps)

def _scatter_add(tgt, idx, src, axis=0):
    return tgt.at[idx].add(src)

def _segment_sum(src, seg, n):
    return jax.ops.segment_sum(src, seg, n)
kernel_name = 'mk_gps_d1_gnn_r8_a0cd42'

def setup_inputs(seed: int=0):
    np.random.seed(seed)
    _w = jnp.asarray

    def _rec_inputs():
        import jax
        import jax.numpy as jnp
        _gk = jax.random.key(seed)
        x = -0.0003713 + 1 * jax.random.normal(jax.random.fold_in(_gk, 1), (6250, 256), jnp.float32)
        src = jax.random.randint(jax.random.fold_in(_gk, 2), (100000,), 0, 6250, jnp.int32)
        dst = jax.random.randint(jax.random.fold_in(_gk, 3), (100000,), 0, 6250, jnp.int32)
        _o = jnp.argsort(dst, stable=True)
        src = src[_o]
        dst = dst[_o]
        return (x, src, dst)
    x, src, dst = _rec_inputs()

    def _L0_gnn_setup():
        import jax, jax.numpy as jnp
        import numpy as np
        N_NODES = 6250
        key = jax.random.key(seed)
        k1, k2, k3 = jax.random.split(key, 3)
        x = jax.random.normal(k1, (N_NODES, 256), dtype=jnp.float32)
        W = jax.random.normal(k2, (256, 256), dtype=jnp.float32) * (1.0 / np.sqrt(256))
        edge_index = jax.random.randint(k3, (2, 200000), 0, N_NODES, dtype=jnp.int64)
        return {'x': x, 'W': W, 'edge_index': edge_index}
    _L0_gnn_all = _L0_gnn_setup()
    _L0_gnn_in = {k: v for k, v in _L0_gnn_all.items() if k in ('W',)}
    del _L0_gnn_all

    def _L0_mix_setup():
        import jax, jax.numpy as jnp
        import numpy as np
        import math
        EMBED = 256
        HEADS = 4
        HEAD_DIM = EMBED // HEADS
        OUT_DIM = 256
        LN_EPS = 1e-05

        def _qkv_init(key):
            spread = math.sqrt(3.0 / EMBED)
            gain, delta = (0.01, 0.01)
            w = jax.random.uniform(key, (EMBED, EMBED), minval=-spread, maxval=spread) * gain
            return w + delta * jnp.eye(EMBED, dtype=w.dtype)

        def _layer_norm(x, g, b):
            mu = jnp.mean(x, axis=-1, keepdims=True)
            var = jnp.mean(jnp.square(x - mu), axis=-1, keepdims=True)
            return (x - mu) * jax.lax.rsqrt(var + LN_EPS) * g + b

        def _split_heads(x, B, S):
            return x.reshape(B, S, HEADS, HEAD_DIM).transpose(0, 2, 1, 3)
        key = jax.random.key(seed)
        ks = jax.random.split(key, 6)
        seq = jax.random.normal(ks[0], (4, 1024, EMBED), dtype=jnp.float32)
        wq = _qkv_init(ks[1])
        wk = _qkv_init(ks[2])
        wv = _qkv_init(ks[3])
        bound = 1.0 / math.sqrt(EMBED)
        wo = jax.random.uniform(ks[4], (OUT_DIM, EMBED), minval=-bound, maxval=bound)
        bo = jax.random.uniform(ks[5], (OUT_DIM,), minval=-bound, maxval=bound)
        ln_k_g = jnp.ones((HEAD_DIM,), jnp.float32)
        ln_k_b = jnp.zeros((HEAD_DIM,), jnp.float32)
        ln_v_g = jnp.ones((HEAD_DIM,), jnp.float32)
        ln_v_b = jnp.zeros((HEAD_DIM,), jnp.float32)
        return {'seq': seq, 'wq': wq, 'wk': wk, 'wv': wv, 'wo': wo, 'bo': bo, 'ln_k_g': ln_k_g, 'ln_k_b': ln_k_b, 'ln_v_g': ln_v_g, 'ln_v_b': ln_v_b}
    _L0_mix_all = _L0_mix_setup()
    _L0_mix_in = {k: v for k, v in _L0_mix_all.items() if k in ('wq', 'wk', 'wv', 'wo', 'bo', 'ln_k_g', 'ln_k_b', 'ln_v_g', 'ln_v_b')}
    del _L0_mix_all

    def _L0_ffn_setup():
        import jax, jax.numpy as jnp
        import numpy as np
        B, N, D = (16, 512, 256)
        NUM_EXPERTS, TOP_K, HEADS = (4, 2, 4)
        N_EDGES = 131072
        LN_EPS = 1e-05

        def _layernorm(x, g, b):
            mu = x.mean(-1, keepdims=True)
            var = ((x - mu) ** 2).mean(-1, keepdims=True)
            return (x - mu) * jax.lax.rsqrt(var + LN_EPS) * g + b

        def _forward(x, edge_index, W_gat, att_src, att_dst, b_gat, ln_gamma, ln_beta, W1, b1, W2, b2):
            Bc, Nc, Dc = x.shape
            M = Bc * Nc
            x_flat = x.reshape(M, Dc)
            h = (x_flat @ W_gat).reshape(M, HEADS, NUM_EXPERTS)
            loops = jnp.arange(M, dtype=edge_index.dtype)
            src = jnp.concatenate([edge_index[0], loops])
            dst = jnp.concatenate([edge_index[1], loops])
            a_src = (h * att_src).sum(-1)
            a_dst = (h * att_dst).sum(-1)
            e = jax.nn.leaky_relu(a_src[src] + a_dst[dst], negative_slope=0.2)
            e_max = jax.ops.segment_max(e, dst, num_segments=M)
            ee = jnp.exp(e - e_max[dst])
            denom = jax.ops.segment_sum(ee, dst, num_segments=M)
            alpha = ee / (denom[dst] + 1e-16)
            msg = h[src] * alpha[:, :, None]
            agg = jax.ops.segment_sum(msg, dst, num_segments=M).reshape(M, HEADS * NUM_EXPERTS) + b_gat
            scores = _layernorm(agg, ln_gamma, ln_beta).reshape(M, HEADS, NUM_EXPERTS).mean(1)
            scores = scores.reshape(Bc, Nc, NUM_EXPERTS)
            topk_s, topk_i = jax.lax.top_k(scores, TOP_K)
            w = jax.nn.softmax(topk_s, axis=-1)
            out = jnp.zeros_like(x)
            for ei in range(NUM_EXPERTS):
                g = jnp.where(topk_i == ei, w, 0.0).sum(-1)
                hh = jax.nn.gelu(x @ W1[ei] + b1[ei], approximate=False)
                out = out + g[..., None] * (hh @ W2[ei] + b2[ei])
            return out
        key = jax.random.key(seed)
        ks = jax.random.split(key, 8)
        s = 0.05
        return {'x': jax.random.normal(ks[0], (B, N, D), jnp.float32), 'W_gat': jax.random.normal(ks[1], (D, HEADS * NUM_EXPERTS), jnp.float32) * s, 'att_src': jax.random.normal(ks[2], (HEADS, NUM_EXPERTS), jnp.float32) * s, 'att_dst': jax.random.normal(ks[3], (HEADS, NUM_EXPERTS), jnp.float32) * s, 'b_gat': jnp.zeros((HEADS * NUM_EXPERTS,), jnp.float32), 'ln_gamma': jnp.ones((HEADS * NUM_EXPERTS,), jnp.float32), 'ln_beta': jnp.zeros((HEADS * NUM_EXPERTS,), jnp.float32), 'W1': jax.random.normal(ks[4], (NUM_EXPERTS, D, 2 * D), jnp.float32) * s, 'b1': jnp.zeros((NUM_EXPERTS, 2 * D), jnp.float32), 'W2': jax.random.normal(ks[5], (NUM_EXPERTS, 2 * D, D), jnp.float32) * s, 'b2': jnp.zeros((NUM_EXPERTS, D), jnp.float32), 'edge_index': jax.random.randint(ks[6], (2, N_EDGES), 0, B * N, jnp.int32)}
    _L0_ffn_all = _L0_ffn_setup()
    _L0_ffn_in = {k: v for k, v in _L0_ffn_all.items() if k in ('W_gat', 'att_src', 'att_dst', 'b_gat', 'ln_gamma', 'ln_beta', 'W1', 'b1', 'W2', 'b2', 'edge_index')}
    del _L0_ffn_all
    return {'x': x, 'src': src, 'dst': dst, 'L0_gnn_W': _L0_gnn_in['W'], 'L0_mix_wq': _L0_mix_in['wq'], 'L0_mix_wk': _L0_mix_in['wk'], 'L0_mix_wv': _L0_mix_in['wv'], 'L0_mix_wo': _L0_mix_in['wo'], 'L0_mix_bo': _L0_mix_in['bo'], 'L0_mix_ln_k_g': _L0_mix_in['ln_k_g'], 'L0_mix_ln_k_b': _L0_mix_in['ln_k_b'], 'L0_mix_ln_v_g': _L0_mix_in['ln_v_g'], 'L0_mix_ln_v_b': _L0_mix_in['ln_v_b'], 'L0_ffn_W_gat': _L0_ffn_in['W_gat'], 'L0_ffn_att_src': _L0_ffn_in['att_src'], 'L0_ffn_att_dst': _L0_ffn_in['att_dst'], 'L0_ffn_b_gat': _L0_ffn_in['b_gat'], 'L0_ffn_ln_gamma': _L0_ffn_in['ln_gamma'], 'L0_ffn_ln_beta': _L0_ffn_in['ln_beta'], 'L0_ffn_W1': _L0_ffn_in['W1'], 'L0_ffn_b1': _L0_ffn_in['b1'], 'L0_ffn_W2': _L0_ffn_in['W2'], 'L0_ffn_b2': _L0_ffn_in['b2'], 'L0_ffn_edge_index': _L0_ffn_in['edge_index']}

def reference(x, src, dst, L0_gnn_W, L0_mix_wq, L0_mix_wk, L0_mix_wv, L0_mix_wo, L0_mix_bo, L0_mix_ln_k_g, L0_mix_ln_k_b, L0_mix_ln_v_g, L0_mix_ln_v_b, L0_ffn_W_gat, L0_ffn_att_src, L0_ffn_att_dst, L0_ffn_b_gat, L0_ffn_ln_gamma, L0_ffn_ln_beta, L0_ffn_W1, L0_ffn_b1, L0_ffn_W2, L0_ffn_b2, L0_ffn_edge_index):
    import jax
    import jax.numpy as jnp

    def _L0_gnn_ref(x, W, edge_index):
        import jax, jax.numpy as jnp
        import numpy as np
        N_NODES = 6250
        N = x.shape[0]
        src, dst = (edge_index[0], edge_index[1])
        h = x @ W
        deg = jax.ops.segment_sum(jnp.ones_like(dst, dtype=h.dtype), dst, num_segments=N)
        deg_inv_sqrt = jnp.where(deg > 0, jax.lax.rsqrt(jnp.maximum(deg, 1)), 0.0)
        norm = deg_inv_sqrt[src] * deg_inv_sqrt[dst]
        msgs = h[src] * norm[:, None]
        out = jax.ops.segment_sum(msgs, dst, num_segments=N)
        return out

    def _L0_mix_ref(seq, wq, wk, wv, wo, bo, ln_k_g, ln_k_b, ln_v_g, ln_v_b):
        import jax, jax.numpy as jnp
        import numpy as np
        import math
        EMBED = 256
        HEADS = 4
        HEAD_DIM = EMBED // HEADS
        OUT_DIM = 256
        LN_EPS = 1e-05

        def _qkv_init(key):
            spread = math.sqrt(3.0 / EMBED)
            gain, delta = (0.01, 0.01)
            w = jax.random.uniform(key, (EMBED, EMBED), minval=-spread, maxval=spread) * gain
            return w + delta * jnp.eye(EMBED, dtype=w.dtype)

        def _layer_norm(x, g, b):
            mu = jnp.mean(x, axis=-1, keepdims=True)
            var = jnp.mean(jnp.square(x - mu), axis=-1, keepdims=True)
            return (x - mu) * jax.lax.rsqrt(var + LN_EPS) * g + b

        def _split_heads(x, B, S):
            return x.reshape(B, S, HEADS, HEAD_DIM).transpose(0, 2, 1, 3)
        B, S, _ = seq.shape
        q = _split_heads(seq @ wq.T, B, S)
        k = _split_heads(seq @ wk.T, B, S)
        v = _split_heads(seq @ wv.T, B, S)
        k = _layer_norm(k, ln_k_g, ln_k_b)
        v = _layer_norm(v, ln_v_g, ln_v_b)
        kv = jnp.einsum('bhsd,bhse->bhde', k, v) / S
        ga = jnp.einsum('bhsd,bhde->bhse', q, kv)
        ga = ga.transpose(0, 2, 1, 3).reshape(B, S, EMBED)
        return ga @ wo.T + bo

    def _L0_ffn_ref(x, W_gat, att_src, att_dst, b_gat, ln_gamma, ln_beta, W1, b1, W2, b2, edge_index):
        import jax, jax.numpy as jnp
        import numpy as np
        B, N, D = (16, 512, 256)
        NUM_EXPERTS, TOP_K, HEADS = (4, 2, 4)
        N_EDGES = 131072
        LN_EPS = 1e-05

        def _layernorm(x, g, b):
            mu = x.mean(-1, keepdims=True)
            var = ((x - mu) ** 2).mean(-1, keepdims=True)
            return (x - mu) * jax.lax.rsqrt(var + LN_EPS) * g + b

        def _forward(x, edge_index, W_gat, att_src, att_dst, b_gat, ln_gamma, ln_beta, W1, b1, W2, b2):
            Bc, Nc, Dc = x.shape
            M = Bc * Nc
            x_flat = x.reshape(M, Dc)
            h = (x_flat @ W_gat).reshape(M, HEADS, NUM_EXPERTS)
            loops = jnp.arange(M, dtype=edge_index.dtype)
            src = jnp.concatenate([edge_index[0], loops])
            dst = jnp.concatenate([edge_index[1], loops])
            a_src = (h * att_src).sum(-1)
            a_dst = (h * att_dst).sum(-1)
            e = jax.nn.leaky_relu(a_src[src] + a_dst[dst], negative_slope=0.2)
            e_max = jax.ops.segment_max(e, dst, num_segments=M)
            ee = jnp.exp(e - e_max[dst])
            denom = jax.ops.segment_sum(ee, dst, num_segments=M)
            alpha = ee / (denom[dst] + 1e-16)
            msg = h[src] * alpha[:, :, None]
            agg = jax.ops.segment_sum(msg, dst, num_segments=M).reshape(M, HEADS * NUM_EXPERTS) + b_gat
            scores = _layernorm(agg, ln_gamma, ln_beta).reshape(M, HEADS, NUM_EXPERTS).mean(1)
            scores = scores.reshape(Bc, Nc, NUM_EXPERTS)
            topk_s, topk_i = jax.lax.top_k(scores, TOP_K)
            w = jax.nn.softmax(topk_s, axis=-1)
            out = jnp.zeros_like(x)
            for ei in range(NUM_EXPERTS):
                g = jnp.where(topk_i == ei, w, 0.0).sum(-1)
                hh = jax.nn.gelu(x @ W1[ei] + b1[ei], approximate=False)
                out = out + g[..., None] * (hh @ W2[ei] + b2[ei])
            return out
        return _forward(x, edge_index, W_gat, att_src, att_dst, b_gat, ln_gamma, ln_beta, W1, b1, W2, b2)
    edge_index = jnp.stack([src, dst])
    xn = _layernorm(x, axis=-1)
    x = x + _L0_gnn_ref(xn, L0_gnn_W, edge_index) + _L0_mix_ref(xn[None], L0_mix_wq, L0_mix_wk, L0_mix_wv, L0_mix_wo, L0_mix_bo, L0_mix_ln_k_g, L0_mix_ln_k_b, L0_mix_ln_v_g, L0_mix_ln_v_b)[0]
    x = x + _L0_ffn_ref(_layernorm(x, axis=-1)[None], L0_ffn_W_gat, L0_ffn_att_src, L0_ffn_att_dst, L0_ffn_b_gat, L0_ffn_ln_gamma, L0_ffn_ln_beta, L0_ffn_W1, L0_ffn_b1, L0_ffn_W2, L0_ffn_b2, L0_ffn_edge_index)[0]
    return x

_drawn_inputs = setup_inputs


def setup_inputs(seed=0):
    import zlib

    import numpy as np

    out = dict(_drawn_inputs(seed))
    spreads = {'L0_mix_ln_k_g': (1.0, 0.6),
     'L0_mix_ln_k_b': (0.0, 0.8),
     'L0_mix_ln_v_g': (1.0, 0.6),
     'L0_mix_ln_v_b': (0.0, 0.8),
     'L0_ffn_b_gat': (0.0, 0.1),
     'L0_ffn_ln_gamma': (1.0, 0.2),
     'L0_ffn_ln_beta': (0.0, 0.1),
     'L0_ffn_b1': (0.0, 0.1),
     'L0_ffn_b2': (0.0, 0.1)}
    factors = {'L0_mix_wq': 4.762, 'L0_mix_wk': 5.215, 'L0_mix_wv': 3.626, 'L0_mix_wo': 3.773}
    for name, (base, spread) in spreads.items():
        noise = np.random.default_rng([zlib.crc32(name.encode()), seed]).standard_normal(out[name].shape)
        drawn = base * np.exp(spread * noise) if base else spread * noise
        out[name] = jnp.asarray(drawn.astype(out[name].dtype))
    for name, factor in factors.items():
        out[name] = (out[name] * factor).astype(out[name].dtype)
    return out
```

```python
import concourse.bass as bass
from concourse import mybir
from contextlib import ExitStack

F32 = mybir.dt.float32
I32 = mybir.dt.int32
ALU = mybir.AluOpType
ACT = mybir.ActivationFunctionType
AX = mybir.AxisListType
REDUCE_MAX = bass.bass_isa.ReduceOp.max

P = 128
NODES = 6250
D = 256
W = -(-NODES // P)
SLOTS = W + 1
PADDED = P * W
FULL = PADDED // W - 1
LAST = NODES - FULL * W
EDGES_GNN = 100000
EDGES_GAT = 131072
SORTED = 1 << 17
F = SORTED // P
ID_BITS = 13
NO_NODE = (1 << ID_BITS) - 1
KEY_BASE = 0x40000000
ROUNDS = 32
CHUNK = 4
RING = 4
GAT_RING = 8
PAIRS = (W - 1) // 2
CHUNKS = 512
ZERO_ROW = PADDED
HEADS, EXPERTS, TOP = 4, 4, 2
GATV = HEADS * (EXPERTS + 1)
GATW = GATV + 2 * HEADS
HID = 512
MIX_HEADS, HEAD_DIM = 4, 64
EPS = 1e-5
GROUP = 7
BIG_DEGREE = float(1 << 24)

C_ID, C_SIGN, C_NODE, C_IOTA, C_Q = 0, 128, 138, 138 + SLOTS, 138 + SLOTS + 64
C_END = C_Q + CHUNKS // P


def link_on(eng, sem):
    n = [0]

    def link(*steps):
        for s in steps:
            s.then_inc(sem, 1)
            n[0] += 1
        eng.wait_ge(sem, n[0])

    return link


def build(nc, x, src, dst, gat_edges, gnn_w, wq, wk_t, wv_t, wo_t, bo, lnkv, gat_w, att, gat_vec,
          w1, b1, w2, b2, consts, out, debug=None):
    top = ExitStack()
    stack = [top]

    def sb(name, shape, dt=F32):
        return stack[-1].enter_context(nc.sbuf_tensor(name, shape, dt))

    def pb(name, shape, dt=F32):
        return stack[-1].enter_context(nc.psum_tensor(name, shape, dt))

    def sem(name):
        return top.enter_context(nc.semaphore(name))

    def sems(*names):
        return [sem(n) for n in names]

    def scope():
        stack.append(ExitStack())

    def leave():
        stack.pop().close()

    def ds(i, n=1):
        return bass.ds(i, n)

    def flat(ap):
        return ap.rearrange("p a b -> p (a b)")

    def row_index(tile, w):
        return bass.IndirectOffsetOnAxis(ap=tile[:, w:w + 1], axis=0)

    tab_gnn = nc.dram_tensor("tab_gnn", [PADDED + 1, D], F32).ap()
    agg_gnn = nc.dram_tensor("agg_gnn", [PADDED, D], F32).ap()
    tab_gat = nc.dram_tensor("tab_gat", [PADDED + 1, GATW], F32).ap()
    y_first = nc.dram_tensor("y_first", [P, EXPERTS * D], F32).ap()
    y_rest = nc.dram_tensor("y_rest", [PAIRS, P, 2 * EXPERTS * D], F32).ap()

    def edge_list(tag, search, space, rows, per_signal):
        t = dict(tag=tag, search=search, samples=SORTED // search, per_signal=per_signal)
        t["V"] = [space[:, 0:F], space[:, F:2 * F]]
        t["T"] = space[:, 2 * F:3 * F]
        t["si"], t["di"] = (space[:, i * F:(i + 1) * F].bitcast(I32) for i in (3, 4))
        t["dst"], t["src"] = t["T"], t["V"][0]
        t["rows"] = rows.rearrange("p (s k) -> p s k", k=search)
        t["dst_rows"] = nc.dram_tensor("dst_rows" + tag, [SORTED // search, search], F32).ap()
        t["src_rows"] = nc.dram_tensor("src_rows" + tag, [SORTED + ROUNDS, ROUNDS], F32).ap()
        t["lists_d"] = nc.dram_tensor("lists_d" + tag, [2, CHUNKS], I32).ap()
        for n in ("cleared", "loaded", "swap_asked", "swapped", "lists_ready", "lists_stored",
                  "samples_known", "samples_spread", "rows_known"):
            t[n] = sem(n + tag)
        t["rows_got"] = [sem(f"rows_got{i}{tag}") for i in range(SLOTS // per_signal)]
        for n in ("src_known", "src_got", "cap_ready", "most_ready", "list_ready", "list_stored", "list_loaded",
                  "plan_step"):
            t[n] = sem(n + tag)
        return t

    def sort_sync(sp, t, load_keys):
        sp.wait_ge(t["cleared"], 1)
        load_keys(sp, t["si"], t["di"], t["loaded"])

    def swap_sync(sp, t):
        n = 0
        for k, bits in ((16, (5,)), (17, (6, 5))):
            for bit in bits:
                n += 1
                sp.wait_ge(t["swap_asked"], n)
                a, b = t["swaps"][n - 1]
                size = 1 << bit
                for p in range(0, P, size):
                    q = p ^ size
                    sp.dma_start(b[p:p + size, :], a[q:q + size, :]).then_inc(t["swapped"], 16)

    def sort_vector(dve, link, t, between=None):
        V, T, si, di = t["V"], t["T"], t["si"], t["di"]
        link(dve.memset(si, 0), dve.memset(di, NO_NODE))
        dve.sem_inc(t["cleared"], 1)
        dve.wait_ge(t["loaded"], 32)
        link(dve.tensor_scalar(si, si, NODES - 1, None, ALU.min),
             dve.tensor_scalar(di, di, NO_NODE, None, ALU.min))
        link(dve.tensor_scalar(di, di, ID_BITS, KEY_BASE, ALU.logical_shift_left, ALU.bitwise_or))
        link(dve.tensor_tensor(V[1].bitcast(I32), si, di, ALU.bitwise_or))
        link(dve.tensor_scalar(V[0], V[1], sign(0), None, ALU.mult))

        def compare(a, b, d, flip=False):
            va = a.rearrange("p (n two d) -> p n two d", two=2, d=d)
            vb = b.rearrange("p (n two d) -> p n two d", two=2, d=d)
            lo = va[:, :, 0, :]
            hi = va[:, :, 1, ::-1] if flip else va[:, :, 1, :]
            to = vb[:, :, 1, ::-1] if flip else vb[:, :, 1, :]
            link(dve.tensor_tensor(vb[:, :, 0, :], lo, hi, ALU.min),
                 dve.tensor_tensor(to, lo, hi, ALU.max))

        a, b, c = V[0], V[1], T
        for k in range(1, 11):
            compare(a, b, 1 << (k - 1), True)
            a, b = b, a
            for j in range(k - 2, -1, -1):
                compare(a, b, 1 << j)
                a, b = b, a
            if k == 9 and between:
                between()
        t["swaps"], dmas = [], 0
        for k in range(11, 18):
            link(dve.tensor_scalar(b, a, sign(k - 10), None, ALU.mult))
            a, b = b, a
            for bit in range(k - 11, 4, -1):
                t["swaps"].append((a, b))
                dve.sem_inc(t["swap_asked"], 1)
                link(dve.tensor_scalar(c, a, sign(bit + 3), None, ALU.mult))
                dmas += P >> bit
                dve.wait_ge(t["swapped"], 16 * dmas)
                link(dve.scalar_tensor_tensor(a, b, sign(bit + 3), c, ALU.mult, ALU.min))
                link(dve.tensor_scalar(b, a, sign(bit + 3), None, ALU.mult))
                a, b = b, a
            link(dve.transpose(b, a))
            a, b = b, a
            for j in range(min(k - 11, 4), -1, -1):
                compare(a, b, 1 << j)
                a, b = b, a
            link(dve.transpose(b, a))
            a, b = b, a
            for j in range(9, -1, -1):
                compare(a, b, 1 << j)
                a, b = b, a
        keys = a.bitcast(I32)
        link(dve.tensor_scalar(di, keys, ID_BITS, NO_NODE, ALU.logical_shift_right, ALU.bitwise_and),
             dve.tensor_scalar(si, keys, NO_NODE, None, ALU.bitwise_and))
        link(dve.tensor_copy(t["dst"], di), dve.tensor_copy(t["src"], si))
        dve.sem_inc(t["lists_ready"], 1)

    def lists_sync(sp, t):
        sp.wait_ge(t["lists_ready"], 1)
        sp.dma_start(t["dst_rows"].rearrange("(p a) b -> p (a b)", p=P), t["dst"]).then_inc(t["lists_stored"], 16)
        sp.wait_ge(zero_filled, 1)
        for b in range(ROUNDS):
            sp.dma_start(bass.AP(t["src_rows"].tensor, ROUNDS + b * (SORTED + ROUNDS - 1), [[F, P], [1, F]]),
                         t["src"]).then_inc(t["lists_stored"], 16)
        sp.dma_start(bass.AP(t["src_rows"].tensor, ROUNDS + SORTED, [[SORTED + ROUNDS - 1, ROUNDS], [1, ROUNDS - 1]]),
                     zero[:, 0:ROUNDS - 1]).then_inc(t["lists_stored"], 16)
        sp.dma_start(t["src_rows"][0:1, :], zero[0:1, :]).then_inc(t["lists_stored"], 16)
        sp.wait_ge(t["lists_stored"], 16 * (ROUNDS + 3))

    def samples_tensor(pe, t):
        pe.wait_ge(t["samples_known"], 1)
        for c in range(t["samples"] // P):
            mm = pe.matmul(t["bc"][:, c * P:(c + 1) * P], ones[:, :], t["diag"][:, c, :], start=True, stop=True)
        mm.then_inc(t["samples_spread"], 1)

    def samples_vector(dve, link, t):
        n, search = t["samples"], t["search"]
        link(*[dve.tensor_scalar(t["diag"][:, c, :], ident, t["dst"][:, c * search:c * search + 1], None, ALU.mult)
               for c in range(n // P)])
        dve.sem_inc(t["samples_known"], 1)
        dve.wait_ge(t["samples_spread"], 1)
        for g in range(SLOTS // 10):
            w0 = g * 10
            for w in range(w0, w0 + 10):
                link(dve.tensor_scalar(t["junk"], t["bc"][:, :], node_id[:, w:w + 1], 0.0,
                                       ALU.is_lt, ALU.add, accum_out=row_f[:, w:w + 1]))
            s = slice(w0, w0 + 10)
            link(dve.tensor_scalar(row_f[:, s], row_f[:, s], -1.0, 0.0, ALU.add, ALU.max))
            link(dve.tensor_copy(row_i[:, s], row_f[:, s]))
            dve.sem_inc(t["rows_known"], 1)

    def search_gpsimd(pool, t):
        pool.wait_ge(t["lists_stored"], 16 * (ROUNDS + 3))
        for w in range(SLOTS):
            if w % 10 == 0:
                pool.wait_ge(t["rows_known"], w // 10 + 1)
            signal = t["rows_got"][w // t["per_signal"]]
            pool.indirect_dma_start(t["rows"][:, w, :], None, t["dst_rows"],
                                    row_index(row_i, w)).then_inc(signal, 16)

    def degrees_vector(dve, link, t, with_root):
        search = t["search"]
        for w in range(SLOTS):
            if w % t["per_signal"] == 0:
                dve.wait_ge(t["rows_got"][w // t["per_signal"]], 16 * t["per_signal"])
            link(dve.tensor_scalar(t["junk"][:, 0:search], t["rows"][:, w, :], node_id[:, w:w + 1], 0.0,
                                   ALU.is_lt, ALU.add, accum_out=below[:, w:w + 1]))
        link(dve.scalar_tensor_tensor(first[:, :], row_f[:, :], float(search), below[:, :], ALU.mult, ALU.add))
        link(dve.tensor_tensor(deg[:, :], first[:, 1:SLOTS], first[:, 0:W], ALU.subtract))
        if with_root:
            link(dve.tensor_scalar(row_f[:, 0:W], deg[:, :], 1.0, None, ALU.max))
            dve.sem_inc(dis_in, 1)
            dve.wait_ge(dis_root, 1)
            link(dve.reciprocal(kw[:, 0:W], below[:, 0:W]))
            link(dve.tensor_scalar(row_f[:, 0:W], deg[:, :], 0.0, None, ALU.is_gt))
            link(dve.tensor_tensor(dis[:, :], kw[:, 0:W], row_f[:, 0:W], ALU.mult))
            dve.sem_inc(dis_ok, 1)
        link(dve.memset(ks[0][:, :], BIG_DEGREE))
        link(dve.scalar_tensor_tensor(ks[0][:, 0:W], deg[:, :], 64.0, iota[:, 0:W], ALU.mult, ALU.add))
        a, b = ks
        for k in range(1, 7):
            for j in range(k - 1, -1, -1):
                flip = j == k - 1
                va = a[:, :].rearrange("p (n two d) -> p n two d", two=2, d=1 << j)
                vb = b[:, :].rearrange("p (n two d) -> p n two d", two=2, d=1 << j)
                hi = va[:, :, 1, ::-1] if flip else va[:, :, 1, :]
                to = vb[:, :, 1, ::-1] if flip else vb[:, :, 1, :]
                link(dve.tensor_tensor(vb[:, :, 0, :], va[:, :, 0, :], hi, ALU.min),
                     dve.tensor_tensor(to, va[:, :, 0, :], hi, ALU.max))
                a, b = b, a
        link(dve.tensor_copy(ki[:, :], a[:, :]))
        link(dve.tensor_scalar(ki[:, :], ki[:, :], 63, None, ALU.bitwise_and))
        link(dve.tensor_copy(kw[:, :], ki[:, :]))
        link(dve.tensor_tensor(b[:, :], a[:, :], kw[:, :], ALU.subtract))
        link(dve.tensor_scalar(left[:, :], b[:, 0:W], 1.0 / 64, None, ALU.mult))
        dve.sem_inc(t["cap_ready"], 1)
        hot = t["hot"]
        link(dve.tensor_tensor(hot, kw[:, 0:W].unsqueeze(2).to_broadcast([P, W, W]),
                               iota[:, 0:W].unsqueeze(1).to_broadcast([P, W, W]), ALU.is_equal))
        link(dve.tensor_tensor(hot, hot, first[:, 0:W].unsqueeze(1).to_broadcast([P, W, W]), ALU.mult))
        link(dve.tensor_reduce(b[:, 0:W], hot, AX.X, ALU.add))
        link(dve.tensor_copy(ki[:, 0:W], b[:, 0:W]))
        link(dve.tensor_scalar(row_i[:, 0:W], ki[:, 0:W], ROUNDS - 1, None, ALU.bitwise_and),
             dve.tensor_scalar(ki[:, 0:W], ki[:, 0:W], 5, None, ALU.logical_shift_right))
        link(dve.tensor_copy(row_f[:, 0:W], row_i[:, 0:W]), dve.tensor_copy(run[:, :], ki[:, 0:W]))
        link(dve.tensor_scalar(copy[:, :], row_f[:, 0:W], float(SORTED // ROUNDS + 1), 1.0, ALU.mult, ALU.add),
             dve.tensor_scalar(b[:, 0:W], kw[:, 0:W], node_id[:, 0:1], None, ALU.add))
        link(dve.tensor_copy(node[:, :], b[:, 0:W]))

    def sources_vector(dve, link, t):
        link(dve.tensor_scalar(prow_f[:, :], run[:, :], float(SORTED // ROUNDS - 1), None, ALU.min))
        link(dve.tensor_tensor(prow_f[:, :], prow_f[:, :], copy[:, :], ALU.add))
        link(dve.tensor_copy(prow_i[:, :], prow_f[:, :]))
        dve.sem_inc(t["src_known"], 1)

    def plan_vector(dve, link, t, per, least):
        dve.wait_ge(t["most_ready"], 1)
        link(dve.tensor_reduce(sc[0][:, 0:1], most[:, :], AX.X, ALU.max))
        link(dve.tensor_scalar(sc[0][:, 0:1], sc[0][:, 0:1], float(ROUNDS - 1), float(ROUNDS), ALU.add, ALU.max))
        link(dve.tensor_copy(nch_i[:, 0:1], sc[0][:, 0:1]))
        link(dve.tensor_scalar(passes_i[:, :], nch_i[:, 0:1], 5, None, ALU.logical_shift_right))
        link(dve.tensor_scalar(most[:, :], most[:, :], float(ROUNDS), float(CHUNK - 1), ALU.min, ALU.add))
        link(dve.tensor_copy(nch_i[:, :], most[:, :]))
        link(dve.tensor_scalar(nch_i[:, :], nch_i[:, :], 2, None, ALU.logical_shift_right))
        link(dve.tensor_copy(nch[:, :], nch_i[:, :]))
        link(dve.tensor_copy(sc[0][:, :], nch[:, :]))
        a, b = sc
        d = 1
        while d < W:
            link(dve.tensor_copy(b[:, 0:d], a[:, 0:d]),
                 dve.tensor_tensor(b[:, d:W], a[:, d:W], a[:, 0:W - d], ALU.add))
            a, b = b, a
            d *= 2
        for c in range(CHUNKS // P):
            link(dve.tensor_scalar(b[:, :], a[:, :], q_id[:, c:c + 1], 0.0, ALU.is_le, ALU.add,
                                   accum_out=slot_f[:, c:c + 1]))
            link(dve.scalar_tensor_tensor(b[:, :], a[:, :], q_id[:, c:c + 1], nch[:, :], ALU.is_le, ALU.mult,
                                          accum_out=off_f[:, c:c + 1]))
        link(dve.tensor_tensor(off_f[:, :], q_id, off_f[:, :], ALU.subtract))
        link(dve.tensor_scalar(off_f[:, :], off_f[:, :], float(CHUNK), None, ALU.mult))
        link(dve.scalar_tensor_tensor(off_f[:, :], slot_f[:, :], float(ROUNDS), off_f[:, :], ALU.mult, ALU.add))
        link(dve.tensor_scalar(off_f[:, :], off_f[:, :], float(W * ROUNDS), None, ALU.min))
        link(dve.tensor_copy(lists_i[:, 0, :], slot_f[:, :]), dve.tensor_copy(lists_i[:, 1, :], off_f[:, :]))
        link(dve.tensor_scalar(b[:, 0:1], a[:, W - 1:W], float(per - 1), float(per * least), ALU.add, ALU.max))
        link(dve.tensor_copy(nch_i[:, 0:1], b[:, 0:1]))
        link(dve.tensor_scalar(iters_i[:, :], nch_i[:, 0:1], per.bit_length() - 1, None, ALU.logical_shift_right))
        dve.sem_inc(t["list_ready"], 1)

    def indices_vector(dve, link, t):
        link(dve.tensor_tensor(idx[:, 0:W, :], iota[:, 0:ROUNDS].unsqueeze(1).to_broadcast([P, W, ROUNDS]),
                               left[:, :].unsqueeze(2).to_broadcast([P, W, ROUNDS]), ALU.is_lt))
        dve.wait_ge(t["src_got"], 16 * W)
        link(dve.scalar_tensor_tensor(raw[:, :, :], raw[:, :, :], -float(ZERO_ROW), idx[:, 0:W, :], ALU.add, ALU.mult))
        link(dve.tensor_scalar(idx[:, 0:W, :], raw[:, :, :], float(ZERO_ROW), None, ALU.add),
             dve.memset(idx[:, W:SLOTS, :], float(ZERO_ROW)))
        link(dve.tensor_scalar(left[:, :], left[:, :], -float(ROUNDS), 0.0, ALU.add, ALU.max),
             dve.tensor_scalar(run[:, :], run[:, :], 1.0, None, ALU.add))

    def most_gpsimd(pool, t):
        pool.wait_ge(t["cap_ready"], 1)
        pool.partition_all_reduce(most[:, :], left[:, :], P, REDUCE_MAX).then_inc(t["most_ready"], 1)

    def sources_gpsimd(pool, t):
        pool.wait_ge(t["src_known"], 1)
        for w in range(W):
            pool.indirect_dma_start(raw[:, w, :], None, t["src_rows"], row_index(prow_i, w)).then_inc(t["src_got"], 16)

    def plan_sync(sp, t):
        sp.wait_ge(t["list_ready"], 1)
        for h in range(2):
            sp.dma_start(t["lists_d"][h].rearrange("(c p) -> p c", p=P).unsqueeze(2), lists_i[:, h, :].unsqueeze(2),
                         allow_slow_non_contiguous=True).then_inc(t["list_stored"], 16)
        sp.wait_ge(t["list_stored"], 32)
        sp.dma_start(lists[0:1, :], t["lists_d"].rearrange("h q -> (h q)").unsqueeze(0)).then_inc(t["list_loaded"], 16)
        sp.wait_ge(t["list_loaded"], 16)

    PASS_SEMS = ("src_known", "src_got", "cap_ready", "most_ready", "list_ready", "list_stored", "list_loaded",
                 "plan_step")

    def more_passes(t, body_sems, per, body):
        every = [t[n].num for n in PASS_SEMS] + [s.num for v in body_sems.values() for s in (v if isinstance(v, list) else [v])]
        lo, hi = min(every), max(every) + 1
        assert len(every) == hi - lo, "the semaphores of a pass are a block"
        passes = nc.values_load(passes_i[0:1, 0:1], min_val=1, max_val=SORTED // ROUNDS)
        with nc.If(passes > 1):
            with nc.Fori(1, passes):
                nc.all_engine_barrier()
                nc.gpsimd.dma_reset(range(lo, hi))
                nc.gpsimd.sem_clear(range(lo, hi))
                nc.all_engine_barrier()
                with nc.Block() as block:
                    @block.vector
                    def _(dve):
                        link = link_on(dve, t["plan_step"])
                        dve.sem_inc(t["cap_ready"], 1)
                        sources_vector(dve, link, t)
                        plan_vector(dve, link, t, per, 1)
                        indices_vector(dve, link, t)

                    @block.gpsimd
                    def _(pool):
                        most_gpsimd(pool, t)
                        sources_gpsimd(pool, t)

                    @block.sync
                    def _(sp):
                        plan_sync(sp, t)
                with nc.Block() as block:
                    body(block)

    def iterations(eng, per=RING):
        return eng.value_load(iters_i[0:1, 0:1], min_val=1, max_val=-(-W * ROUNDS // (CHUNK * per)))

    def slot_of(eng, it, c, per=RING):
        return eng.value_load(lists[0:1, ds(it * per + c, 1)], min_val=0, max_val=W)

    def stage_indices(act, it, c, after, stage, staged, per=RING):
        at = it * per + (CHUNKS + after * per + c)
        off = act.value_load(lists[0:1, ds(at, 1)] if not isinstance(at, int) else lists[0:1, at:at + 1],
                             min_val=0, max_val=W * ROUNDS)
        act.activation(stage[:, c, :], flat(idx[:, :, :])[:, ds(off, CHUNK)], ACT.Copy).then_inc(staged, 1)

    def gather_chunk(pool, it, c, stage, rows, table, free, staged, landed):
        pool.wait_ge(free[c], it + 1)
        pool.wait_ge(staged[c], it + 1)
        pool.nop(nofuse=True)
        for r in range(CHUNK):
            pool.indirect_dma_start(rows[:, c, r, :], None, table, row_index(stage[:, c, :], r)).then_inc(landed[c], 16)

    with top:
        cst = sb("cst", [P, C_END])
        ident = cst[:, C_ID:C_ID + P]
        node_id = cst[:, C_NODE:C_NODE + SLOTS]
        iota = cst[:, C_IOTA:C_IOTA + 64]
        q_id = cst[:, C_Q:C_END]

        def sign(k):
            return cst[:, C_SIGN + k:C_SIGN + k + 1]

        X = sb("X", [P, W, D])
        acc = sb("acc", [P, SLOTS, D])
        XT = sb("XT", [P, 2, PADDED])
        dis = sb("dis", [P, W])
        Mx = sb("Mx", [P, 2, D])
        zero, ones = sb("zero", [ROUNDS, ROUNDS]), sb("ones", [P, P])
        idx = sb("idx", [P, SLOTS, ROUNDS])
        raw = sb("raw", [P, W, ROUNDS])
        lists = sb("lists", [1, 2 * CHUNKS], I32)
        row_f, row_i = sb("row_f", [P, SLOTS]), sb("row_i", [P, SLOTS], I32)
        below, first, deg = sb("below", [P, SLOTS]), sb("first", [P, SLOTS]), sb("deg", [P, W])
        ks = [sb(f"ks{i}", [P, 64]) for i in range(2)]
        ki, kw = sb("ki", [P, 64], I32), sb("kw", [P, 64])
        left, run, copy, most, nch, prow_f = (sb(n, [P, W]) for n in ("left", "run", "copy", "most", "nch", "prow_f"))
        sc = [sb(f"sc{i}", [P, W]) for i in range(2)]
        node, prow_i, nch_i = (sb(n, [P, W], I32) for n in ("node", "prow_i", "nch_i"))
        slot_f, off_f = sb("slot_f", [P, CHUNKS // P]), sb("off_f", [P, CHUNKS // P])
        lists_i = sb("lists_i", [P, 2, CHUNKS // P], I32)
        passes_i, iters_i = sb("passes_i", [P, 1], I32), sb("iters_i", [P, 1], I32)

        accf, Xf = flat(acc[:, :, :]), flat(X[:, :, :])
        te = edge_list("e", 256, accf[:, 0:5 * F], accf[:, 0:SLOTS * 256], 10)
        gnn_body = dict(free=[sem(f"g_free{c}") for c in range(RING)], staged=[sem(f"g_staged{c}") for c in range(RING)],
                        landed=[sem(f"g_landed{c}") for c in range(RING)], summed=sem("g_summed"), moved=sem("g_moved"))

        zero_filled, dis_in, dis_root, dis_ok = sems("zero_filled", "dis_in", "dis_root", "dis_ready")

        scope()
        s_in = [sem(f"x_loaded{g}") for g in range(W // GROUP)]
        c_in, x_zero, eps_ok, ln_s, mean_ok, root_ok, rinv_ok, shift_ok, normed, turned, moved, sort_s = sems(
            "consts_loaded", "x_zeroed", "eps_ready", "ln_step", "ln_mean", "ln_root", "ln_rinv", "ln_shift",
            "ln_normed", "ln_turned", "ln_moved", "sort_step")
        ssum, ssq, root, rinv, shift = (sb(n, [P, W]) for n in ("ssum", "ssq", "root", "rinv", "shift"))
        eps = sb("eps", [P, 1])
        sq = sb("sq", [P, D])
        xn = sb("xn", [P, 2, D])
        tp = [pb(f"tp{i}", [P, 2, P]) for i in range(2)]

        def load_gnn(sp, si, di, s):
            n = 125
            sp.dma_start(si[0:n, 0:EDGES_GNN // n], src.rearrange("(p f) -> p f", p=n)).then_inc(s, 16)
            sp.dma_start(di[0:n, 0:EDGES_GNN // n], dst.rearrange("(p f) -> p f", p=n)).then_inc(s, 16)

        def load_x(sp, signals):
            for g in range(W // GROUP):
                s = slice(g * GROUP, (g + 1) * GROUP)
                e = min(LAST, (g + 1) * GROUP)
                sp.dma_start(X[0:FULL, s, :], x[0:FULL * W, :].rearrange("(p w) d -> p w d", w=W)[:, s, :]).then_inc(signals[g], 16)
                if e > g * GROUP:
                    sp.dma_start(X[FULL:P, g * GROUP:e, :],
                                 x[FULL * W + g * GROUP:FULL * W + e, :].unsqueeze(0)).then_inc(signals[g], 16)

        def x_landed(eng, signals, g):
            eng.wait_ge(signals[g], 32 if LAST > g * GROUP else 16)

        with nc.Block() as block:
            @block.vector
            def _(dve):
                link = link_on(dve, sort_s)
                dve.wait_ge(c_in, 16)

                def between():
                    dve.wait_ge(root_ok, 1)
                    link(dve.reciprocal(rinv[:, :], root[:, :]))
                    dve.sem_inc(rinv_ok, 1)
                sort_vector(dve, link, te, between)

            @block.sync
            def _(sp):
                sp.dma_start(cst[:, :], consts).then_inc(c_in, 16)
                sort_sync(sp, te, load_gnn)
                sp.wait_ge(x_zero, 1)
                load_x(sp, s_in)
                swap_sync(sp, te)

            @block.gpsimd
            def _(pool):
                pool.memset(X[96:P, :, :], 0.0).then_inc(x_zero, 1)
                pool.wait_ge(x_zero, 1)
                pool.memset(eps[:, :], EPS).then_inc(eps_ok, 1)
                pool.wait_ge(eps_ok, 1)
                pool.wait_ge(rinv_ok, 1)
                pool.tensor_tensor(shift[:, :], ssum[:, :], rinv[:, :], ALU.mult).then_inc(shift_ok, 1)

            @block.scalar
            def _(act):
                act.wait_ge(x_zero, 1)
                act.wait_ge(eps_ok, 1)
                for g in range(W // GROUP):
                    x_landed(act, s_in, g)
                    for w in range(g * GROUP, (g + 1) * GROUP):
                        if w:
                            act.wait_ge(ln_s, w)
                        act.activation(sq[:, :], X[:, w, :], ACT.Copy, accum_out=ssum[:, w:w + 1]).then_inc(ln_s, 1)
                act.wait_ge(ln_s, W)
                act.mul(ssum[:, :], ssum[:, :], -1.0 / D).then_inc(mean_ok, 1)
                act.wait_ge(mean_ok, 1)
                for w in range(W):
                    act.activation(sq[:, :], X[:, w, :], ACT.Square, bias=ssum[:, w:w + 1],
                                   accum_out=ssq[:, w:w + 1]).then_inc(ln_s, 1)
                    act.wait_ge(ln_s, W + w + 1)
                act.activation(root[:, :], ssq[:, :], ACT.Sqrt, bias=eps[:, 0:1], scale=1.0 / D).then_inc(root_ok, 1)
                act.wait_ge(shift_ok, 1)
                act.wait_ge(rinv_ok, 1)
                for w in range(W + 1):
                    if w < W:
                        if w >= 2:
                            act.wait_ge(turned, w - 1)
                        act.activation(xn[:, w % 2, :], X[:, w, :], ACT.Identity,
                                       bias=shift[:, w:w + 1], scale=rinv[:, w:w + 1]).then_inc(normed, 1)
                    if w:
                        act.wait_ge(turned, w)
                        act.activation(XT[:, :, (w - 1) * P:w * P], tp[(w - 1) % 2][:, :, :], ACT.Copy).then_inc(moved, 1)

            @block.tensor
            def _(pe):
                pe.wait_ge(c_in, 16)
                for w in range(W):
                    pe.wait_ge(normed, w + 1)
                    if w >= 2:
                        pe.wait_ge(moved, w - 1)
                    for c in range(2):
                        mm = pe.transpose(tp[w % 2][:, c, :], xn[:, w % 2, c * P:(c + 1) * P], ident)
                    mm.then_inc(turned, 1)
        leave()
        if debug and debug[0] == "xt":
            return debug[1](nc, sem, out, XT)

        scope()
        te["rows"] = flat(X[:, :, :])[:, 0:W * D].rearrange("p (s k) -> p s k", k=256)
        spare = sb("spare_rows", [P, 256])
        te["rows_last"] = spare
        te["diag"] = sb("diag", [P, 4, P])
        te["junk"] = sb("junk", [P, 512])[:, :]
        te["bc"] = pb("bc", [P, 512])
        te["hot"] = accf[:, 5 * F:5 * F + W * W].rearrange("p (a b) -> p a b", b=W)
        gw = sb("gw", [P, 2, D])
        hb = [sb(f"hb{i}", [P, GROUP, D]) for i in range(2)]
        zrow = sb("zrow", [1, D])
        hp = [pb(f"hp{i}", [P, D]) for i in range(2)]
        gw_in, h_mm, h_ok, z_ok, step2, acc0 = sems("gw_loaded", "h_product", "h_scaled", "zero_row", "degree_step", "acc_zeroed")
        h_out = [sem(f"h_stored{i}") for i in range(2)]

        class Rows:
            def __getitem__(self, key):
                _, w, cols = key
                return te["x_rows"][:, w, cols] if w < W else te["rows_last"][:, cols]
        te["x_rows"], te["rows"] = te["rows"], Rows()
        with nc.Block() as block:
            @block.sync
            def _(sp):
                for c in range(2):
                    sp.dma_start(gw[:, c, :], gnn_w[c * P:(c + 1) * P, :]).then_inc(gw_in, 16)
                lists_sync(sp, te)
                plan_sync(sp, te)
                sp.wait_ge(z_ok, 1)
                sp.dma_start(tab_gnn[ZERO_ROW:ZERO_ROW + 1, :], zrow[:, :]).then_inc(gw_in, 16)
                sp.wait_ge(gw_in, 48)

            @block.gpsimd
            def _(pool):
                search_gpsimd(pool, te)
                most_gpsimd(pool, te)
                sources_gpsimd(pool, te)
                pool.wait_ge(acc0, 1)

            @block.vector
            def _(dve):
                link = link_on(dve, step2)
                link(dve.memset(zrow[:, :], 0.0), dve.memset(zero[:, :], 0.0), dve.memset(ones[:, :], 1.0))
                dve.sem_inc(z_ok, 1)
                dve.sem_inc(zero_filled, 1)
                samples_vector(dve, link, te)
                degrees_vector(dve, link, te, True)
                sources_vector(dve, link, te)
                plan_vector(dve, link, te, RING, W)
                dve.wait_ge(te["lists_stored"], 16 * (ROUNDS + 3))
                link(dve.memset(accf[:, :], 0.0))
                dve.sem_inc(acc0, 1)
                indices_vector(dve, link, te)

            @block.tensor
            def _(pe):
                samples_tensor(pe, te)
                pe.wait_ge(gw_in, 32)
                for w in range(W):
                    if w >= 2:
                        pe.wait_ge(h_ok, w - 1)
                    for c in range(2):
                        mm = pe.matmul(hp[w % 2][:, :], XT[:, c, w * P:(w + 1) * P], gw[:, c, :], start=(c == 0), stop=(c == 1))
                    mm.then_inc(h_mm, 1)

            @block.scalar
            def _(act):
                act.wait_ge(dis_in, 1)
                act.activation(below[:, 0:W], row_f[:, 0:W], ACT.Sqrt).then_inc(dis_root, 1)
                act.wait_ge(dis_ok, 1)
                tv = tab_gnn[0:PADDED, :].rearrange("(p w) d -> p w d", w=W)
                for w in range(W):
                    g, b = w // GROUP, w // GROUP % 2
                    if w % GROUP == 0 and g >= 2:
                        act.wait_ge(h_out[b], 16 * (g // 2))
                    act.wait_ge(h_mm, w + 1)
                    act.activation(hb[b][:, w % GROUP, :], hp[w % 2][:, :], ACT.Copy, scale=dis[:, w:w + 1]).then_inc(h_ok, 1)
                    if w % GROUP == GROUP - 1:
                        act.wait_ge(h_ok, w + 1)
                        act.dma_start(tv[:, g * GROUP:(g + 1) * GROUP, :], hb[b][:, :, :]).then_inc(h_out[b], 16)
                for b in range(2):
                    act.wait_ge(h_out[b], 16 * ((W // GROUP + 1 - b) // 2))
        leave()
        if debug and debug[0] == "deg":
            return debug[1](nc, sem, out, dis, left, node)

        scope()
        ta = edge_list("a", 128, Xf[:, 0:5 * F], Xf[:, 5 * F:5 * F + SLOTS * 128], SLOTS)
        ta["diag"] = Xf[:, 5 * F:5 * F + 8 * P].rearrange("p (c q) -> p c q", q=P)
        ta["junk"] = Xf[:, 3 * F:4 * F]
        ta["hot"] = Xf[:, 0:W * W].rearrange("p (a b) -> p a b", b=W)
        gat_body = dict(free=[sem(f"a_free{h}") for h in range(2)], staged=[sem(f"a_staged{h}") for h in range(2)],
                        landed=[sem(f"a_landed{q}") for q in range(GAT_RING)], step=sem("a_step"),
                        exp_in=sem("a_exp_in"), exp_out=sem("a_exp_out"))
        rows = sb("rows", [P, RING, CHUNK, D])
        stage = sb("stage", [P, RING, CHUNK], I32)
        sp_ps = [pb(f"sum_ps{i}", [P, D]) for i in range(2)]
        free, staged, landed, summed, moved = (gnn_body[n] for n in ("free", "staged", "landed", "summed", "moved"))

        def load_gat(sp, si, di, s):
            sp.dma_start(si, gat_edges[0].rearrange("(p f) -> p f", p=P)).then_inc(s, 16)
            sp.dma_start(di, gat_edges[1].rearrange("(p f) -> p f", p=P)).then_inc(s, 16)

        def sum_chunk(pe, it, c):
            n = it * RING + c
            at = slot_of(pe, it, c)
            pe.wait_ge(landed[c], (it + 1) * (16 * CHUNK))
            pe.wait_ge(moved, n + 1)
            for r in range(CHUNK):
                mm = pe.matmul(sp_ps[c % 2][:, :], ident, rows[:, c, r, :], start=(r == 0), stop=False)
            mm.then_inc(free[c], 1)
            pe.wait_ge(moved, n + 2)
            pe.matmul(sp_ps[c % 2][:, :], ident, flat(acc[:, ds(at, 1), :]), start=False, stop=True).then_inc(summed, 1)

        def move_chunk(act, it, c, next_too=True):
            at = slot_of(act, it, c)
            act.wait_ge(summed, it * RING + (c + 1))
            act.activation(flat(acc[:, ds(at, 1), :]), sp_ps[c % 2][:, :], ACT.Copy).then_inc(moved, 1)
            stage_indices(act, it, c, 1, stage, staged[c])

        def sum_begin(act):
            act.sem_inc(moved, 2)
            for c in range(RING):
                stage_indices(act, 0, c, 0, stage, staged[c])

        def sum_free(pe):
            for c in range(RING):
                pe.sem_inc(free[c], 1)

        def sum_body(block):
            @block.scalar
            def _(act):
                sum_begin(act)
                with act.Fori(0, iterations(act)) as it:
                    for c in range(RING):
                        move_chunk(act, it, c)

            @block.gpsimd
            def _(pool):
                with pool.Fori(0, iterations(pool)) as it:
                    for c in range(RING):
                        gather_chunk(pool, it, c, stage, rows, tab_gnn, free, staged, landed)

            @block.tensor
            def _(pe):
                sum_free(pe)
                with pe.Fori(0, iterations(pe)) as it:
                    for c in range(RING):
                        sum_chunk(pe, it, c)

        scope()
        wkv = sb("wkv", [P, 2, 2 * D])
        gkv, bkv = sb("gkv", [P, 2 * D]), sb("bkv", [P, 2 * D])
        wmean = sb("wmean", [P, 16])
        xw = sb("xw", [P, 2, 2, P])
        kv = sb("kv", [P, 2, 2 * D])
        sq = sb("kv_sq", [P, 2, 2 * D])
        ssq, rt, rv = (sb(n, [P, 2, 8]) for n in ("kv_ssq", "kv_root", "kv_rinv"))
        wq_sb, wo_sb = (Xf[:, 5 * F + i * 512:5 * F + (i + 1) * 512].rearrange("p (c d) -> p c d", c=2) for i in (0, 1))
        bd = Xf[:, 5 * F + 1024:5 * F + 1280].rearrange("p (c d) -> p c d", c=2)
        bw = Xf[:, 5 * F + 1536:5 * F + 2048].rearrange("p (c d) -> p c d", c=2)
        kvp = [pb(f"kvp{i}", [P, 2 * D]) for i in range(2)]
        kvs = pb("kvs", [P, 2, 512])
        ta["bc"] = flat(kvs[:, :, :])
        (w_in, mix_s, centred, xw_ok, product, squared, var_ok, root_ok, kv_ok, kv_used, kv_done, bd_ok, bw_mm, bw_ok,
         m_mm, sort_s, mid) = sems(
            "mix_loaded", "mix_step", "kv_centred", "xw_ready", "kv_product", "kv_squared", "kv_var", "kv_root",
            "kv_ready", "kv_used", "kv_summed", "bd_ready", "bw_product", "bw_ready", "m_product", "sort2_step", "mid_signal")
        FULL_ITS, ALL_ITS, MID_ITS = (LAST - 1) // 2, (W - 1) // 2, W - 1

        with nc.Block() as block:
            @block.vector
            def _(dve):
                link = link_on(dve, mix_s)
                dve.wait_ge(w_in, 160)
                g = wkv[:, :, :].rearrange("p c (h e) -> p (c h) e", e=HEAD_DIM)
                link(dve.tensor_reduce(wmean[:, :], g, AX.X, ALU.add), dve.memset(bd, 0.0))
                link(dve.tensor_scalar(wmean[:, :], wmean[:, :], 1.0 / HEAD_DIM, None, ALU.mult))
                link(dve.tensor_tensor(g, g, wmean[:, :].unsqueeze(2).to_broadcast([P, 16, HEAD_DIM]), ALU.subtract))
                dve.sem_inc(centred, 1)
                STEPS = 4

                def normalize(w, b):
                    k = w * STEPS
                    heads = lambda a: a.rearrange("p (h e) -> p h e", e=HEAD_DIM)
                    dve.wait_ge(squared, w + 1)
                    dve.tensor_reduce(ssq[:, b, :], heads(sq[:, b, :]), AX.X, ALU.add).then_inc(mid, 1)
                    dve.wait_ge(mid, k + 1)
                    dve.tensor_scalar(ssq[:, b, :], ssq[:, b, :], 1.0 / HEAD_DIM, EPS, ALU.mult, ALU.add).then_inc(var_ok, 1)
                    dve.wait_ge(root_ok, w + 1)
                    dve.reciprocal(rv[:, b, :], rt[:, b, :]).then_inc(mid, 1)
                    dve.wait_ge(mid, k + 2)
                    if not (isinstance(w, int) and w == 0):
                        dve.wait_ge(kv_used, w)
                    dve.tensor_tensor(heads(kv[:, b, :]), heads(kvp[b][:, :]),
                                      rv[:, b, :].unsqueeze(2).to_broadcast([P, 8, HEAD_DIM]), ALU.mult).then_inc(mid, 1)
                    dve.wait_ge(mid, k + 3)
                    dve.tensor_tensor(kv[:, b, :], kv[:, b, :], gkv[:, :], ALU.mult).then_inc(mid, 1)
                    dve.wait_ge(mid, k + 4)
                    dve.tensor_tensor(kv[:, b, :], kv[:, b, :], bkv[:, :], ALU.add).then_inc(kv_ok, 1)

                normalize(0, 0)
                with dve.Fori(0, ALL_ITS) as it:
                    normalize(it * 2 + 1, 1)
                    normalize(it * 2 + 2, 0)
                dve.wait_ge(kv_used, W)
                for q in range(2):
                    for h in range(2):
                        s = slice(h * 64, h * 64 + 64)
                        dve.tensor_scalar(bd[s, q, s], kvs[s, q, s], 1.0 / NODES, None, ALU.mult).then_inc(bd_ok, 1)
                dve.wait_ge(bw_mm, 1)
                dve.tensor_copy(bw, kvs[:, :, 0:D]).then_inc(bw_ok, 1)
                dve.wait_ge(m_mm, 1)
                link2 = link_on(dve, sort_s)
                link2(dve.tensor_copy(Mx[:, :, :], kvs[:, :, D:2 * D]))
                sort_vector(dve, link2, ta)
                samples_vector(dve, link2, ta)

            @block.sync
            def _(sp):
                for c in range(2):
                    sp.dma_start(wkv[:, c, 0:D], wk_t[c * P:(c + 1) * P, :]).then_inc(w_in, 16)
                    sp.dma_start(wkv[:, c, D:2 * D], wv_t[c * P:(c + 1) * P, :]).then_inc(w_in, 16)
                    sp.dma_start(wq_sb[:, c, :], wq[c * P:(c + 1) * P, :]).then_inc(w_in, 16)
                    sp.dma_start(wo_sb[:, c, :], wo_t[c * P:(c + 1) * P, :]).then_inc(w_in, 16)
                sp.dma_start(gkv[:, :], lnkv[0:1, :].to_broadcast([P, 2 * D])).then_inc(w_in, 16)
                sp.dma_start(bkv[:, :], lnkv[1:2, :].to_broadcast([P, 2 * D])).then_inc(w_in, 16)
                sort_sync(sp, ta, load_gat)
                swap_sync(sp, ta)
                lists_sync(sp, ta)

            @block.gpsimd
            def _(pool):
                n = iterations(pool)
                with pool.Fori(0, MID_ITS) as it:
                    for c in range(RING):
                        gather_chunk(pool, it, c, stage, rows, tab_gnn, free, staged, landed)
                search_gpsimd(pool, ta)
                with pool.Fori(MID_ITS, n) as it:
                    for c in range(RING):
                        gather_chunk(pool, it, c, stage, rows, tab_gnn, free, staged, landed)

            @block.scalar
            def _(act):
                n = iterations(act)

                def copy_window(w, b):
                    act.wait_ge(product, w) if isinstance(w, int) and w == 0 else None
                    if not (isinstance(w, int) and w == 0):
                        act.wait_ge(product, w - 1 + 1)
                    act.activation(xw[:, b, :, :], XT[:, :, ds(w * P, P)] if not isinstance(w, int) else XT[:, :, w * P:(w + 1) * P],
                                   ACT.Copy).then_inc(xw_ok, 1)

                def square(w, b):
                    act.wait_ge(product, w + 1)
                    act.activation(sq[:, b, :], kvp[b][:, :], ACT.Square).then_inc(squared, 1)

                def take_root(w, b):
                    act.wait_ge(var_ok, w + 1)
                    act.activation(rt[:, b, :], ssq[:, b, :], ACT.Sqrt).then_inc(root_ok, 1)

                sum_begin(act)
                copy_window(0, 0)
                square(0, 0)
                take_root(0, 0)
                with act.Fori(0, ALL_ITS) as it:
                    w = it * 2 + 1
                    copy_window(w, 1)
                    move_chunk(act, it, 0)
                    square(w, 1)
                    copy_window(w + 1, 0)
                    move_chunk(act, it, 1)
                    take_root(w, 1)
                    square(w + 1, 0)
                    move_chunk(act, it, 2)
                    take_root(w + 1, 0)
                    move_chunk(act, it, 3)
                with act.Fori(ALL_ITS, n) as it:
                    for c in range(RING):
                        move_chunk(act, it, c)

            @block.tensor
            def _(pe):
                n = iterations(pe)

                def product_of(w, b):
                    pe.wait_ge(xw_ok, w + 1)
                    if not (isinstance(w, int) and w == 0):
                        pe.wait_ge(kv_ok, w)
                    for c in range(2):
                        mm = pe.matmul(kvp[b][:, :], xw[:, b, c, :], wkv[:, c, :], start=(c == 0), stop=(c == 1))
                    mm.then_inc(product, 1)

                def sum_kv(w, b, count, first=False, last=False):
                    pe.wait_ge(kv_ok, w + 1)
                    for q in range(2):
                        mm = pe.matmul(kvs[:, q, 0:P], kv[0:count, b, D + q * P:D + (q + 1) * P],
                                       kv[0:count, b, q * P:(q + 1) * P], start=first, stop=last, skip_group_check=True)
                    mm.then_inc(kv_used, 1)

                sum_free(pe)
                pe.wait_ge(centred, 1)
                product_of(0, 0)
                sum_kv(0, 0, P, first=True)
                for i0, i1, count in ((0, FULL_ITS, P), (FULL_ITS, ALL_ITS, FULL)):
                    with pe.Fori(i0, i1) as it:
                        w = it * 2 + 1
                        sum_chunk(pe, it, 0)
                        product_of(w, 1)
                        sum_chunk(pe, it, 1)
                        sum_kv(w, 1, count)
                        product_of(w + 1, 0)
                        sum_chunk(pe, it, 2)
                        sum_chunk(pe, it, 3)
                        sum_kv(w + 1, 0, count)
                pe.wait_ge(bd_ok, 4)
                for q in range(2):
                    mm = pe.matmul(kvs[:, q, 0:D], bd[:, q, :], wo_sb[:, q, :], start=True, stop=True)
                mm.then_inc(bw_mm, 1)
                pe.wait_ge(bw_ok, 1)
                for i in range(2):
                    for q in range(2):
                        mm = pe.matmul(kvs[:, i, D:2 * D], wq_sb[:, q, i * P:(i + 1) * P], bw[:, q, :],
                                       start=(q == 0), stop=(q == 1))
                mm.then_inc(m_mm, 1)
                with pe.Fori(ALL_ITS, MID_ITS - 2) as it:
                    for c in range(RING):
                        sum_chunk(pe, it, c)
                samples_tensor(pe, ta)
                with pe.Fori(MID_ITS - 2, n) as it:
                    for c in range(RING):
                        sum_chunk(pe, it, c)
        leave()
        more_passes(te, gnn_body, RING, sum_body)
        leave()
        if debug and debug[0] == "b3":
            return debug[1](nc, sem, out, acc, Mx, node)

        scope()
        own = sb("own", [P, SLOTS, GATW])
        state = sb("state", [P, SLOTS, GATV])
        top_score = sb("top_score", [P, SLOTS, HEADS])
        scope()
        node_g = sb("node_g", [P, W], I32)
        bo_sb = sb("bo_sb", [1, D])
        stats, mv = sb("stats", [P, W, 6]), sb("mv", [P, W, 2])
        var, root, rinv, shift = (sb(n + "2", [P, W]) for n in ("var", "root", "rinv", "shift"))
        xn = sb("xn2", [P, 2, D])
        wg, att_sb = sb("wg", [P, 2, 16]), sb("att_sb", [P, 2, 16])
        tab, prod = sb("tab", [P, W, GATW]), sb("prod", [P, W, 16])
        zrow = sb("zrow2", [1, GATW])
        mp = [pb(f"mp{i}", [P, D]) for i in range(2)]
        tp = [pb(f"tp2{i}", [P, 2, P]) for i in range(2)]
        hp = pb("hp16", [P, 1024])
        (w_in, node_ok, x_free, x_clear, scattered, xm, x_pre, deg_s, var_ok, root_ok, rinv_ok, normed, turned, moved,
         h16, tab_ok, tab_out, own_in) = sems(
            "gap_loaded", "node_saved", "x_free", "x_cleared", "agg_scattered", "xm_product", "x_added", "gap_step",
            "ln2_var", "ln2_root", "ln2_rinv", "ln2_normed", "ln2_turned", "ln2_moved", "h16_product", "tab_ready",
            "tab_stored", "own_rows")
        groups = W // GROUP

        with nc.Block() as block:
            @block.gpsimd
            def _(pool):
                pool.wait_ge(node_ok, 1)
                for w in range(W):
                    pool.indirect_dma_start(agg_gnn, row_index(node_g, w), acc[:, w, :], None).then_inc(scattered, 16)
                sources_gpsimd(pool, ta)
                most_gpsimd(pool, ta)
                pool.wait_ge(tab_out, 32)
                for w in range(W):
                    pool.indirect_dma_start(own[:, w, :], None, tab_gat, row_index(node, w)).then_inc(own_in, 16)

            @block.vector
            def _(dve):
                link = link_on(dve, deg_s)
                link(dve.tensor_copy(node_g[:, :], node[:, :]))
                dve.sem_inc(node_ok, 1)
                degrees_vector(dve, link, ta, False)
                sources_vector(dve, link, ta)
                dve.memset(X[96:P, LAST:W, :], 0.0).then_inc(x_free, 1)
                link(dve.memset(tab[:, :, :], 1.0), dve.memset(zrow[:, :], 0.0), dve.memset(own[:, W:SLOTS, :], 0.0))
                link(dve.memset(zrow[:, GATV:GATV + HEADS], -1e30))

                def scales(g):
                    s = slice(g * GROUP, (g + 1) * GROUP)
                    dve.wait_ge(root_ok, g + 1)
                    link(dve.reciprocal(rinv[:, s], root[:, s]))
                    link(dve.scalar_tensor_tensor(shift[:, s], mv[:, s, 0], -1.0, rinv[:, s], ALU.mult, ALU.mult))
                    dve.sem_inc(rinv_ok, 1)

                for g in range(groups):
                    s = slice(g * GROUP, (g + 1) * GROUP)
                    dve.wait_ge(s_in[g], 2 * (32 if LAST > g * GROUP else 16) + 16)
                    for w in range(g * GROUP, (g + 1) * GROUP):
                        dve.wait_ge(xm, w + 1)
                        dve.scalar_tensor_tensor(acc[:, w, :], acc[:, w, :], dis[:, w:w + 1], mp[w % 2][:, :],
                                                 ALU.mult, ALU.add).then_inc(x_pre, 1)
                    dve.wait_ge(x_pre, (g + 1) * GROUP)
                    link(dve.tensor_tensor(X[:, s, :], X[:, s, :], acc[:, s, :], ALU.add))
                    link(*[dve.bn_stats(stats[:, w, :], X[:, w, :]) for w in range(g * GROUP, (g + 1) * GROUP)])
                    link(*[dve.bn_aggr(mv[:, w, :], stats[:, w, :]) for w in range(g * GROUP, (g + 1) * GROUP)])
                    link(dve.tensor_scalar(var[:, s], mv[:, s, 1], EPS, None, ALU.add))
                    dve.sem_inc(var_ok, 1)
                    if g:
                        scales(g - 1)
                scales(groups - 1)
                dve.wait_ge(w_in, 16 * 5)
                dve.wait_ge(h16, 1)
                hv = hp[:, 0:W * 16].rearrange("p (w c) -> p w c", c=16)
                to = tab[:, :, 0:GATV].rearrange("p w (h e) -> p w h e", h=HEADS)[:, :, :, 0:EXPERTS]
                link(dve.tensor_copy(to, hv.rearrange("p w (h e) -> p w h e", h=HEADS)))
                for c in range(2):
                    link(dve.tensor_tensor(prod[:, :, :], hv, att_sb[:, c, :].unsqueeze(1).to_broadcast([P, W, 16]), ALU.mult))
                    link(dve.tensor_reduce(tab[:, :, GATV + c * HEADS:GATV + (c + 1) * HEADS],
                                           prod[:, :, :].rearrange("p w (h e) -> p w h e", h=HEADS), AX.X, ALU.add))
                dve.sem_inc(tab_ok, 1)
                plan_vector(dve, link, ta, GAT_RING, PAIRS + 1)
                indices_vector(dve, link, ta)
                dve.wait_ge(own_in, 16 * W)
                link(dve.tensor_copy(state[:, :, :], own[:, :, 0:GATV]),
                     dve.tensor_tensor(top_score[:, :, :], own[:, :, GATV:GATV + HEADS], own[:, :, GATV + HEADS:GATW], ALU.add))
                link(dve.scalar_tensor_tensor(top_score[:, :, :], top_score[:, :, :], 0.2, top_score[:, :, :], ALU.mult, ALU.max))

            @block.sync
            def _(sp):
                sp.dma_start(bo_sb[:, :], bo.unsqueeze(0)).then_inc(w_in, 16)
                for c in range(2):
                    sp.dma_start(wg[:, c, :], gat_w[c * P:(c + 1) * P, :]).then_inc(w_in, 16)
                    sp.dma_start(att_sb[:, c, :], att[c:c + 1, :].to_broadcast([P, 16])).then_inc(w_in, 16)
                sp.wait_ge(x_free, 1)
                load_x(sp, s_in)
                sp.wait_ge(scattered, 16 * W)
                av = agg_gnn.rearrange("(p w) d -> p w d", w=W)
                for g in range(groups):
                    s = slice(g * GROUP, (g + 1) * GROUP)
                    sp.dma_start(acc[:, s, :], av[:, s, :]).then_inc(s_in[g], 16)
                sp.wait_ge(tab_ok, 1)
                sp.dma_start(tab_gat[0:PADDED, :].rearrange("(p w) c -> p w c", w=W), tab[:, :, :]).then_inc(tab_out, 16)
                sp.dma_start(tab_gat[ZERO_ROW:ZERO_ROW + 1, :], zrow[:, :]).then_inc(tab_out, 16)
                sp.wait_ge(tab_out, 32)
                plan_sync(sp, ta)

            @block.tensor
            def _(pe):
                pe.wait_ge(w_in, 16 * 5)

                def h16_of(w):
                    pe.wait_ge(moved, w + 1)
                    for c in range(2):
                        mm = pe.matmul(hp[:, w * 16:(w + 1) * 16], XT[:, c, w * P:(w + 1) * P], wg[:, c, :],
                                       start=(c == 0), stop=(c == 1))
                    return mm

                for g in range(groups + 1):
                    if g < groups:
                        for w in range(g * GROUP, (g + 1) * GROUP):
                            if w >= 2:
                                pe.wait_ge(x_pre, w - 1)
                            for c in range(2):
                                pe.matmul(mp[w % 2][:, :], XT[:, c, w * P:(w + 1) * P], Mx[:, c, :], start=(c == 0), stop=False)
                            pe.matmul(mp[w % 2][:, :], ones[0:1, :], bo_sb[:, :], start=False, stop=True).then_inc(xm, 1)
                    if g:
                        for w in range((g - 1) * GROUP, g * GROUP):
                            pe.wait_ge(normed, w + 1)
                            if w >= 2:
                                pe.wait_ge(moved, w - 1)
                            for c in range(2):
                                mm = pe.transpose(tp[w % 2][:, c, :], xn[:, w % 2, c * P:(c + 1) * P], ident)
                            mm.then_inc(turned, 1)
                            if w:
                                h16_of(w - 1)
                h16_of(W - 1).then_inc(h16, 1)

            @block.scalar
            def _(act):
                for g in range(groups + 1):
                    if g < groups:
                        s = slice(g * GROUP, (g + 1) * GROUP)
                        act.wait_ge(var_ok, g + 1)
                        act.activation(root[:, s], var[:, s], ACT.Sqrt).then_inc(root_ok, 1)
                    if g:
                        act.wait_ge(rinv_ok, g)
                        for w in range((g - 1) * GROUP, g * GROUP):
                            if w >= 2:
                                act.wait_ge(turned, w - 1)
                            act.activation(xn[:, w % 2, :], X[:, w, :], ACT.Identity,
                                           bias=shift[:, w:w + 1], scale=rinv[:, w:w + 1]).then_inc(normed, 1)
                            if w:
                                act.wait_ge(turned, w)
                                act.wait_ge(xm, w)
                                act.activation(XT[:, :, (w - 1) * P:w * P], tp[(w - 1) % 2][:, :, :], ACT.Copy).then_inc(moved, 1)
                act.wait_ge(turned, W)
                act.activation(XT[:, :, (W - 1) * P:W * P], tp[(W - 1) % 2][:, :, :], ACT.Copy).then_inc(moved, 1)
        leave()
        if debug and debug[0] == "gap":
            debug[1](nc, sem, out, X, XT, left, node, state)
            leave()
            return

        HALF = GAT_RING // 2
        scope()
        rows = sb("a_rows", [P, GAT_RING, CHUNK, GATW])
        stage = sb("a_stage", [P, GAT_RING, CHUNK], I32)
        e = sb("a_e", [P, GAT_RING, CHUNK + 1, HEADS])
        high, top_of = (sb(n, [P, GAT_RING, HEADS]) for n in ("a_high", "a_top"))
        pr, part = sb("a_pr", [P, HALF, CHUNK, GATV]), sb("a_part", [P, HALF, GATV])
        free, staged, landed, step, exp_in, exp_out = (gat_body[n] for n in
                                                       ("free", "staged", "landed", "step", "exp_in", "exp_out"))
        PER_HALF = 7 * HALF + 4

        def gather_half(pool, it, h):
            pool.wait_ge(free[h], it + 1)
            pool.wait_ge(staged[h], it * HALF + HALF)
            pool.nop(nofuse=True)
            for q in range(h * HALF, (h + 1) * HALF):
                for r in range(CHUNK):
                    pool.indirect_dma_start(rows[:, q, r, :], None, tab_gat,
                                            row_index(stage[:, q, :], r)).then_inc(landed[q], 16)

        def exp_half(act, it, h):
            qs = slice(h * HALF, (h + 1) * HALF)
            act.wait_ge(exp_in, it * 2 + (h + 1))
            act.activation(e[:, qs, :, :], e[:, qs, :, :], ACT.Exp).then_inc(exp_out, 1)
            for q in range(h * HALF, (h + 1) * HALF):
                stage_indices(act, it, q, 1, stage, staged[h], GAT_RING)

        def attend_half(dve, it, h):
            n = [0]

            def link(*steps):
                for s in steps:
                    s.then_inc(step, 1)
                    n[0] += 1
                dve.wait_ge(step, it * (2 * PER_HALF) + (h * PER_HALF + n[0]))

            q0 = h * HALF
            qs = slice(q0, q0 + HALF)
            at = [slot_of(dve, it, q, GAT_RING) for q in range(q0, q0 + HALF)]
            for q in range(q0, q0 + HALF):
                dve.wait_ge(landed[q], it * (16 * CHUNK) + 16 * CHUNK)
                dve.tensor_tensor(e[:, q, 0:CHUNK, :], rows[:, q, :, GATV:GATV + HEADS],
                                  own[:, ds(at[q - q0], 1), GATV + HEADS:GATW].to_broadcast([P, CHUNK, HEADS]),
                                  ALU.add).then_inc(step, 1)
                n[0] += 1
            dve.wait_ge(step, it * (2 * PER_HALF) + (h * PER_HALF + n[0]))
            link(dve.scalar_tensor_tensor(e[:, qs, 0:CHUNK, :], e[:, qs, 0:CHUNK, :], 0.2, e[:, qs, 0:CHUNK, :],
                                          ALU.mult, ALU.max))
            link(dve.tensor_reduce(high[:, qs, :], e[:, qs, 0:CHUNK, :].rearrange("p q r h -> p q h r"), AX.X, ALU.max))
            for q in range(q0, q0 + HALF):
                m = flat(top_score[:, ds(at[q - q0], 1), :])
                link(dve.tensor_tensor(e[:, q, CHUNK, :], m, m, ALU.max), dve.tensor_tensor(top_of[:, q, :], high[:, q, :], m, ALU.max))
                link(dve.tensor_tensor(m, top_of[:, q, :], top_of[:, q, :], ALU.max))
            link(dve.tensor_tensor(e[:, qs, :, :], e[:, qs, :, :],
                                   top_of[:, qs, :].unsqueeze(2).to_broadcast([P, HALF, CHUNK + 1, HEADS]), ALU.subtract))
            dve.sem_inc(exp_in, 1)
            dve.wait_ge(exp_out, it * 2 + (h + 1))
            for c in range(HALF):
                link(dve.tensor_tensor(pr[:, c, :, :].rearrange("p r (h v) -> p r h v", h=HEADS),
                                       rows[:, q0 + c, :, 0:GATV].rearrange("p r (h v) -> p r h v", h=HEADS),
                                       e[:, q0 + c, 0:CHUNK, :].unsqueeze(3).to_broadcast([P, CHUNK, HEADS, EXPERTS + 1]),
                                       ALU.mult))
            dve.sem_inc(free[h], 1)
            link(dve.tensor_reduce(part[:, :, :], pr[:, :, :, :].rearrange("p c r v -> p c v r"), AX.X, ALU.add))
            for c in range(HALF):
                my = state[:, ds(at[c], 1), :].rearrange("p s (h v) -> p (s h) v", h=HEADS)
                link(dve.tensor_tensor(my, my, e[:, q0 + c, CHUNK, :].unsqueeze(2).to_broadcast([P, HEADS, EXPERTS + 1]), ALU.mult))
                link(dve.tensor_tensor(my, my, part[:, c, :].rearrange("p (h v) -> p h v", h=HEADS), ALU.add))
            assert n[0] == PER_HALF, n[0]

        def attend_free(dve):
            for h in range(2):
                dve.sem_inc(free[h], 1)

        def stage_first(act):
            for q in range(GAT_RING):
                stage_indices(act, 0, q, 0, stage, staged[q // HALF], GAT_RING)

        def gather_all(pool):
            with pool.Fori(0, iterations(pool, GAT_RING)) as it:
                for h in range(2):
                    gather_half(pool, it, h)

        def gat_pass(block):
            @block.scalar
            def _(act):
                stage_first(act)
                with act.Fori(0, iterations(act, GAT_RING)) as it:
                    for h in range(2):
                        exp_half(act, it, h)

            @block.gpsimd
            def _(pool):
                gather_all(pool)

            @block.vector
            def _(dve):
                attend_free(dve)
                with dve.Fori(0, iterations(dve, GAT_RING)) as it:
                    for h in range(2):
                        attend_half(dve, it, h)

        FT = HID // P
        Y = EXPERTS * D
        scope()
        w1_sb = accf[:, 0:4096].rearrange("p (e c f) -> p e c f", e=EXPERTS, c=2)
        w2_sb = accf[:, 4096:8192].rearrange("p (e k d) -> p e k d", e=EXPERTS, k=FT)
        hh = accf[:, 8192:12288].rearrange("p (e k n) -> p e k n", e=EXPERTS, k=FT)
        b1_sb, b2_sb = sb("b1_sb", [P, EXPERTS, FT]), sb("b2_sb", [1, EXPERTS, D])
        y_sb = sb("y_sb", [P, 2, EXPERTS, D])
        hid = [pb(f"hid{i}", [P, 2, 256]) for i in range(4)]
        yp = [pb(f"yp{e_}", [P, 2, D]) for e_ in range(EXPERTS)]
        f_in, hidden_ok, gelu_ok, y_mm, y_ok, y_out, y_in = sems(
            "ffn_loaded", "ffn_hidden", "ffn_gelu", "ffn_product", "ffn_moved", "ffn_stored", "y_loaded")
        in_xt, in_acc = 2 * PADDED // Y, 7
        XTf = flat(XT[:, :, :])
        y_buf = [XTf[:, i * Y:(i + 1) * Y] for i in range(in_xt)] + [accf[:, i * Y:(i + 1) * Y] for i in range(in_acc)]
        PREFETCH = len(y_buf)

        def load_y(sp, w, signal):
            at = y_first if w == 0 else y_rest[(w - 1) // 2, :, (w - 1) % 2 * Y:((w - 1) % 2 + 1) * Y]
            sp.dma_start(y_buf[w % PREFETCH], at).then_inc(signal, 16)

        with nc.Block() as block:
            @block.sync
            def _(sp):
                for x_ in range(EXPERTS):
                    sp.dma_start(w1_sb[:, x_, :, :], w1[x_].rearrange("(c p) f -> p c f", p=P)).then_inc(f_in, 16)
                    sp.dma_start(w2_sb[:, x_, :, :], w2[x_].rearrange("(k p) d -> p k d", p=P)).then_inc(f_in, 16)
                sp.dma_start(b1_sb[:, :, :], b1.rearrange("p (e k) -> p e k", e=EXPERTS)).then_inc(f_in, 16)
                sp.dma_start(b2_sb[:, :, :], b2.unsqueeze(0)).then_inc(f_in, 16)
                sp.wait_ge(y_ok, EXPERTS)
                sp.dma_start(y_first, y_sb[:, 0, :, :].rearrange("p e d -> p (e d)")).then_inc(y_out, 16)
                with sp.Fori(0, PAIRS) as g:
                    sp.wait_ge(y_ok, g * EXPERTS + 2 * EXPERTS)
                    sp.dma_start(y_rest[ds(g, 1), :, :].rearrange("g p n -> p (g n)"),
                                 y_sb[:, :, :, :].rearrange("p v e d -> p (v e d)")).then_inc(y_out, 16)
                sp.wait_ge(y_out, 16 * (PAIRS + 1))
                for w in range(PREFETCH):
                    load_y(sp, w, y_in)
                sp.wait_ge(y_in, 16 * PREFETCH)

            @block.tensor
            def _(pe):
                pe.wait_ge(f_in, 16 * (2 * EXPERTS + 2))

                def hidden(n, e_, first_col, cols):
                    for f in range(FT):
                        bank = e_ % 2 * 2 + f // 2
                        if f % 2 == 0 and not (isinstance(n, int) and n < 2):
                            pe.wait_ge(gelu_ok, (n - 2) * FT + (f + 2))
                        for c in range(2):
                            mm = pe.matmul(hid[bank][:, f % 2, 0:cols], w1_sb[:, e_, c, f * P:(f + 1) * P],
                                           XT[:, c, ds(first_col, cols)], start=(c == 0), stop=(c == 1))
                        mm.then_inc(hidden_ok, 1)

                def output(n, e_, wins):
                    pe.wait_ge(gelu_ok, n * FT + FT)
                    if not (isinstance(n, int) and n < EXPERTS):
                        pe.wait_ge(y_ok, n - (EXPERTS - 1))
                    for v in range(wins):
                        for k in range(FT):
                            pe.matmul(yp[e_][:, v, :], hh[:, e_, k, v * P:(v + 1) * P], w2_sb[:, e_, k, :],
                                      start=(k == 0), stop=False)
                        mm = pe.matmul(yp[e_][:, v, :], ones[0:1, :], b2_sb[:, e_, :], start=False, stop=True)
                    mm.then_inc(y_mm, 1)

                def windows(n0, first_col, wins):
                    hidden(n0, 0, first_col, wins * P)
                    for e_ in range(1, EXPERTS):
                        hidden(n0 + e_, e_, first_col, wins * P)
                        output(n0 + (e_ - 1), e_ - 1, wins)
                    output(n0 + (EXPERTS - 1), EXPERTS - 1, wins)

                windows(0, 0, 1)
                with pe.Fori(0, PAIRS) as g:
                    windows(g * EXPERTS + EXPERTS, g * (2 * P) + P, 2)

            def gelu(act, n, e_, cols):
                if not (isinstance(n, int) and n < EXPERTS):
                    act.wait_ge(y_mm, n - (EXPERTS - 1))
                for f in range(FT):
                    if f % 2 == 0:
                        act.wait_ge(hidden_ok, n * FT + (f + 2))
                    act.activation(hh[:, e_, f, 0:cols], hid[e_ % 2 * 2 + f // 2][:, f % 2, 0:cols], ACT.Gelu,
                                   bias=b1_sb[:, e_, f:f + 1]).then_inc(gelu_ok, 1)

            @block.scalar
            def _(act):
                n = iterations(act, GAT_RING)
                stage_first(act)
                act.wait_ge(f_in, 16 * (2 * EXPERTS + 2))
                for e_ in range(EXPERTS):
                    gelu(act, e_, e_, P)
                with act.Fori(0, PAIRS) as it:
                    for h in range(2):
                        exp_half(act, it, h)
                        for e_ in (2 * h, 2 * h + 1):
                            gelu(act, it * EXPERTS + (EXPERTS + e_), e_, 2 * P)
                with act.Fori(PAIRS, n) as it:
                    for h in range(2):
                        exp_half(act, it, h)

            @block.gpsimd
            def _(pool):
                gather_all(pool)

            @block.vector
            def _(dve):
                n = iterations(dve, GAT_RING)

                def move(k, e_, wins):
                    dve.wait_ge(y_mm, k + 1)
                    dve.tensor_copy(y_sb[:, 0:wins, e_, :], yp[e_][:, 0:wins, :]).then_inc(y_ok, 1)

                attend_free(dve)
                for e_ in range(EXPERTS):
                    move(e_, e_, 1)
                with dve.Fori(0, PAIRS) as it:
                    for h in range(2):
                        attend_half(dve, it, h)
                    dve.wait_ge(y_out, it * 16 + 16)
                    for e_ in range(EXPERTS):
                        move(it * EXPERTS + (EXPERTS + e_), e_, 2)
                with dve.Fori(PAIRS, n) as it:
                    for h in range(2):
                        attend_half(dve, it, h)
        leave()
        more_passes(ta, gat_body, GAT_RING, gat_pass)
        leave()

        scope()
        vec = sb("vec", [P, 3, 16])
        den, ag, sqr = sb("den", [P, W, HEADS]), sb("ag", [P, W, 16]), sb("sqr", [P, W, 16])
        mean, vr, rt = (sb(n, [P, W]) for n in ("g_mean", "g_var", "g_root"))
        sco, rank, ex, gates = (sb(n, [P, W, EXPERTS]) for n in ("sco", "rank", "ex", "gates"))
        less = sb("less", [P, W])
        gate_tmp = accf[:, in_acc * Y:]
        hot, picked = (gate_tmp[:, i * W * W:(i + 1) * W * W].rearrange("p (a b) -> p a b", b=W) for i in range(2))
        v_in, step, a_in, a_out, added, stored = sems("gat_vec_loaded", "gate_step", "gate_act_in", "gate_act_out",
                                                      "expert_added", "stored")
        BATCH = 5
        y_more = [sem(f"y_more{i}") for i in range(-(-(W - PREFETCH) // BATCH))]
        with nc.Block() as block:
            @block.sync
            def _(sp):
                for c in range(3):
                    sp.dma_start(vec[:, c, :], gat_vec[c:c + 1, :].to_broadcast([P, 16])).then_inc(v_in, 16)
                for w in range(PREFETCH, W):
                    sp.wait_ge(added, w - PREFETCH + 1)
                    load_y(sp, w, y_more[(w - PREFETCH) // BATCH])

            @block.scalar
            def _(act):
                act.wait_ge(a_in, 1)
                act.activation(rt[:, :], vr[:, :], ACT.Sqrt).then_inc(a_out, 1)
                act.wait_ge(a_in, 2)
                act.activation(ex[:, :, :], sco[:, :, :], ACT.Exp).then_inc(a_out, 1)
                outs = 0
                for g in range(groups):
                    act.wait_ge(added, (g + 1) * GROUP)
                    s, last = slice(g * GROUP, (g + 1) * GROUP), min(LAST, (g + 1) * GROUP)
                    act.dma_start(out[0:FULL * W, :].rearrange("(p w) d -> p w d", w=W)[:, s, :], X[0:FULL, s, :]).then_inc(stored, 16)
                    outs += 1
                    if last > g * GROUP:
                        act.dma_start(out[FULL * W + g * GROUP:FULL * W + last, :].unsqueeze(0),
                                      X[FULL:P, g * GROUP:last, :]).then_inc(stored, 16)
                        outs += 1
                act.wait_ge(stored, 16 * outs)

            @block.vector
            def _(dve):
                link = link_on(dve, step)
                dve.wait_ge(v_in, 48)
                sv = state[:, 0:W, :].rearrange("p w (h e) -> p w h e", h=HEADS)
                def wide(a):
                    return a[:, :].unsqueeze(2).to_broadcast([P, W, 16])
                def row(c):
                    return vec[:, c, :].unsqueeze(1).to_broadcast([P, W, 16])
                a4 = ag[:, :, :].rearrange("p w (h e) -> p w h e", h=HEADS)
                link(dve.tensor_scalar(den[:, :, :], sv[:, :, :, EXPERTS], 1e-16, None, ALU.add))
                link(dve.reciprocal(den[:, :, :], den[:, :, :]))
                link(dve.tensor_tensor(a4, sv[:, :, :, 0:EXPERTS], den[:, :, :].unsqueeze(3).to_broadcast([P, W, HEADS, EXPERTS]), ALU.mult))
                link(dve.tensor_tensor(ag[:, :, :], ag[:, :, :], row(0), ALU.add))
                link(dve.tensor_reduce(mean[:, :], ag[:, :, :], AX.X, ALU.add))
                link(dve.tensor_scalar(mean[:, :], mean[:, :], 1.0 / 16, None, ALU.mult))
                link(dve.tensor_tensor(ag[:, :, :], ag[:, :, :], wide(mean), ALU.subtract))
                link(dve.tensor_tensor(sqr[:, :, :], ag[:, :, :], ag[:, :, :], ALU.mult))
                link(dve.tensor_reduce(vr[:, :], sqr[:, :, :], AX.X, ALU.add))
                link(dve.tensor_scalar(vr[:, :], vr[:, :], 1.0 / 16, EPS, ALU.mult, ALU.add))
                dve.sem_inc(a_in, 1)
                link(dve.tensor_tensor(hot, iota[:, 0:W].unsqueeze(2).to_broadcast([P, W, W]),
                                       kw[:, 0:W].unsqueeze(1).to_broadcast([P, W, W]), ALU.is_equal))
                dve.wait_ge(a_out, 1)
                link(dve.reciprocal(rt[:, :], rt[:, :]))
                link(dve.tensor_tensor(ag[:, :, :], ag[:, :, :], wide(rt), ALU.mult))
                link(dve.tensor_tensor(ag[:, :, :], ag[:, :, :], row(1), ALU.mult))
                link(dve.tensor_tensor(ag[:, :, :], ag[:, :, :], row(2), ALU.add))
                link(dve.tensor_reduce(sco[:, :, :], ag[:, :, :].rearrange("p w (h e) -> p w e h", h=HEADS), AX.X, ALU.add))
                link(dve.tensor_scalar(sco[:, :, :], sco[:, :, :], 1.0 / HEADS, None, ALU.mult), dve.memset(rank[:, :, :], 0.0))
                for e_ in range(EXPERTS):
                    for f in range(e_):
                        link(dve.tensor_tensor(less[:, :], sco[:, :, f], sco[:, :, e_], ALU.is_ge))
                        link(dve.tensor_tensor(rank[:, :, e_], rank[:, :, e_], less[:, :], ALU.add))
                        link(dve.tensor_tensor(less[:, :], sco[:, :, f], sco[:, :, e_], ALU.is_lt))
                        link(dve.tensor_tensor(rank[:, :, f], rank[:, :, f], less[:, :], ALU.add))
                link(dve.tensor_reduce(mean[:, :], sco[:, :, :], AX.X, ALU.max))
                link(dve.tensor_tensor(sco[:, :, :], sco[:, :, :], mean[:, :].unsqueeze(2).to_broadcast([P, W, EXPERTS]), ALU.subtract))
                dve.sem_inc(a_in, 1)
                dve.wait_ge(a_out, 2)
                link(dve.scalar_tensor_tensor(ex[:, :, :], rank[:, :, :], float(TOP), ex[:, :, :], ALU.is_lt, ALU.mult))
                link(dve.tensor_reduce(mean[:, :], ex[:, :, :], AX.X, ALU.add))
                link(dve.reciprocal(mean[:, :], mean[:, :]))
                link(dve.tensor_tensor(ex[:, :, :], ex[:, :, :], mean[:, :].unsqueeze(2).to_broadcast([P, W, EXPERTS]), ALU.mult))
                for e_ in range(EXPERTS):
                    link(dve.tensor_tensor(picked, hot, ex[:, :, e_].unsqueeze(1).to_broadcast([P, W, W]), ALU.mult))
                    link(dve.tensor_reduce(gates[:, :, e_], picked, AX.X, ALU.add))
                for w in range(W):
                    if w >= PREFETCH:
                        dve.wait_ge(y_more[(w - PREFETCH) // BATCH], 16 * min(BATCH, W - PREFETCH - (w - PREFETCH) // BATCH * BATCH))
                    for e_ in range(EXPERTS):
                        link(dve.scalar_tensor_tensor(X[:, w, :], y_buf[w % PREFETCH][:, e_ * D:(e_ + 1) * D],
                                                      gates[:, w, e_:e_ + 1], X[:, w, :], ALU.mult, ALU.add))
                    dve.sem_inc(added, 1)
        leave()
        leave()


def constants():
    import numpy as np
    c = np.zeros((P, C_END), np.float32)
    p = np.arange(P)
    c[:, C_ID:C_ID + P] = np.eye(P)

    def direction(k):
        return np.where((p >> (k - 10)) & 1, -1.0, 1.0)

    c[:, C_SIGN] = direction(10)
    for k in range(11, 18):
        c[:, C_SIGN + k - 10] = direction(k - 1) * direction(k)
    for bit in (5, 6):
        c[:, C_SIGN + bit + 3] = np.where((p >> bit) & 1, -1.0, 1.0)
    c[:, C_NODE:C_NODE + SLOTS] = p[:, None] * W + np.arange(SLOTS)
    c[:, C_IOTA:C_IOTA + 64] = np.arange(64)
    c[:, C_Q:C_END] = np.arange(CHUNKS // P) * P + p[:, None]
    return c


def lay_out(i):
    import numpy as np
    a = {k: np.ascontiguousarray(v) for k, v in i.items()}
    cat, tile = np.concatenate, np.tile
    m = "L0_mix_"
    f = "L0_ffn_"
    t = lambda v: np.ascontiguousarray(v.T)
    return {
        "x": a["x"], "src": a["src"], "dst": a["dst"], "gat_edges": a[f + "edge_index"],
        "gnn_w": a["L0_gnn_W"], "wq": a[m + "wq"], "wk_t": t(a[m + "wk"]), "wv_t": t(a[m + "wv"]),
        "wo_t": t(a[m + "wo"]), "bo": a[m + "bo"],
        "lnkv": np.stack([cat([tile(a[m + "ln_k_g"], 4), tile(a[m + "ln_v_g"], 4)]),
                          cat([tile(a[m + "ln_k_b"], 4), tile(a[m + "ln_v_b"], 4)])]),
        "gat_w": a[f + "W_gat"],
        "att": np.stack([a[f + "att_src"].reshape(-1), a[f + "att_dst"].reshape(-1)]),
        "gat_vec": np.stack([a[f + "b_gat"], a[f + "ln_gamma"], a[f + "ln_beta"]]),
        "w1": a[f + "W1"], "b1": np.ascontiguousarray(a[f + "b1"].reshape(EXPERTS * HID // P, P).T),
        "w2": a[f + "W2"], "b2": a[f + "b2"], "consts": constants(),
    }


def kernel(**inputs):
    import numpy as np
    import concourse.bacc as bacc
    from concourse.bass_utils import run_bass_kernel_spmd as run

    nc = bacc.Bacc("TRN2", target_bir_lowering=False, num_devices=1)
    arrays, args = {}, []
    for name, a in lay_out(inputs).items():
        arrays["in_" + name] = a
        args.append(nc.dram_tensor("in_" + name, a.shape, mybir.dt.from_np(a.dtype), kind="ExternalInput").ap())
    o = nc.dram_tensor("out", (NODES, D), F32, kind="ExternalOutput").ap()
    build(nc, *args, o)
    r = run(nc, [arrays], core_ids=[0])
    return r.results[0]["out"]
```

```python
import concourse.bass as bass
from concourse import mybir
from contextlib import ExitStack

F32 = mybir.dt.float32
I32 = mybir.dt.int32
ALU = mybir.AluOpType
ACT = mybir.ActivationFunctionType
AX = mybir.AxisListType
REDUCE_MAX = bass.bass_isa.ReduceOp.max

P = 128
NODES = 6250
D = 256
W = -(-NODES // P)
SLOTS = W + 1
PADDED = P * W
FULL = PADDED // W - 1
LAST = NODES - FULL * W
EDGES_GNN = 100000
EDGES_GAT = 131072
SORTED = 1 << 17
F = SORTED // P
ID_BITS = 13
NO_NODE = (1 << ID_BITS) - 1
KEY_BASE = 0x40000000
ROUNDS = 32
CHUNK = 4
RING = 4
GAT_RING = 10
PAIRS = (W - 1) // 2
CHUNKS = 512
ZERO_ROW = PADDED
HEADS, EXPERTS, TOP = 4, 4, 2
GATV = HEADS * (EXPERTS + 1)
GATW = GATV + 2 * HEADS
HID = 512
HEAD_DIM = 64
EPS = 1e-5
GROUP = 7
BIG_DEGREE = float(1 << 24)

C_ID, C_SIGN, C_NODE, C_IOTA, C_Q = 0, 128, 138, 138 + SLOTS, 138 + SLOTS + P
C_END = C_Q + CHUNKS // P


def link_on(eng, sem):
    n = [0]

    def link(*steps):
        for s in steps:
            s.then_inc(sem, 1)
            n[0] += 1
        eng.wait_ge(sem, n[0])

    return link


def build(nc, x, src, dst, gat_edges, gnn_w, wq, wk_t, wv_t, wo_t, bo, lnkv, gat_w, att, gat_vec,
          w1, b1, w2, b2, consts, out, debug=None):
    top = ExitStack()
    stack = [top]

    def sb(name, shape, dt=F32):
        return stack[-1].enter_context(nc.sbuf_tensor(name, shape, dt))

    def pb(name, shape, dt=F32):
        return stack[-1].enter_context(nc.psum_tensor(name, shape, dt))

    def sem(name):
        return top.enter_context(nc.semaphore(name))

    def sems(*names):
        return [sem(n) for n in names]

    def scope():
        stack.append(ExitStack())

    def leave():
        stack.pop().close()

    def ds(i, n=1):
        return bass.ds(i, n)

    def flat(ap):
        return ap.rearrange("p a b -> p (a b)")

    def row_index(tile, w):
        return bass.IndirectOffsetOnAxis(ap=tile[:, w:w + 1], axis=0)

    tab_gnn = nc.dram_tensor("tab_gnn", [PADDED + 1, D], F32).ap()
    agg_gnn = nc.dram_tensor("agg_gnn", [PADDED, D], F32).ap()
    tab_gat = nc.dram_tensor("tab_gat", [PADDED + 1, GATW], F32).ap()
    SEARCH_IT, SOURCES_IT, MIX_IT = 22, 26, 28
    MIX_STEPS = (W - 1) // 3
    MIX_END = MIX_IT + 2 * MIX_STEPS
    y_first = nc.dram_tensor("y_first", [P, EXPERTS * D], F32).ap()
    y_rest = nc.dram_tensor("y_rest", [PAIRS, P, 2 * EXPERTS * D], F32).ap()

    def edge_list(tag, search, space, rows, per_signal):
        t = dict(tag=tag, search=search, samples=SORTED // search, per_signal=per_signal)
        t["V"] = [space[:, 0:F], space[:, F:2 * F]]
        t["T"] = space[:, 2 * F:3 * F]
        t["si"], t["di"] = (space[:, i * F:(i + 1) * F].bitcast(I32) for i in (3, 4))
        t["dst"], t["src"] = t["T"], t["V"][0]
        t["rows"] = rows.rearrange("p (s k) -> p s k", k=search)
        t["dst_rows"] = nc.dram_tensor("dst_rows" + tag, [SORTED // search, search], F32).ap()
        t["src_rows"] = nc.dram_tensor("src_rows" + tag, [SORTED + ROUNDS, ROUNDS], F32).ap()
        t["lists_d"] = nc.dram_tensor("lists_d" + tag, [2, CHUNKS], I32).ap()
        for n in ("left", "run", "copy"):
            t[n] = sb(n + tag, [P, W])
        t["kw"], t["node"] = sb("kw" + tag, [P, 64]), sb("node" + tag, [P, W], I32)
        t["idx"], t["lists"] = sb("idx" + tag, [P, SLOTS, ROUNDS]), sb("lists" + tag, [1, 2 * CHUNKS], I32)
        t["passes_i"], t["iters_i"] = sb("passes_i" + tag, [P, 1], I32), sb("iters_i" + tag, [P, 1], I32)
        for n in ("cleared", "loaded", "swap_asked", "swapped", "lists_ready", "dst_stored", "lists_stored",
                  "samples_known", "samples_spread", "rows_known"):
            t[n] = sem(n + tag)
        t["rows_got"] = [sem(f"rows_got{i}{tag}") for i in range(SLOTS // per_signal)]
        for n in ("src_known", "src_got", "cap_ready", "most_ready", "list_ready", "list_stored", "list_loaded",
                  "plan_step"):
            t[n] = sem(n + tag)
        return t

    def sort_sync(sp, t, load_keys):
        sp.wait_ge(t["cleared"], 1)
        load_keys(sp, t["si"], t["di"], t["loaded"])

    def swap_sync(sp, t):
        n = 0
        for k, bits in ((16, (5,)), (17, (6, 5))):
            for bit in bits:
                n += 1
                sp.wait_ge(t["swap_asked"], n)
                a, b = t["swaps"][n - 1]
                size = 1 << bit
                for p in range(0, P, size):
                    q = p ^ size
                    sp.dma_start(b[p:p + size, :], a[q:q + size, :]).then_inc(t["swapped"], 16)

    def sort_vector(dve, link, t, between=None):
        V, T, si, di = t["V"], t["T"], t["si"], t["di"]
        link(dve.memset(si, 0), dve.memset(di, NO_NODE))
        dve.sem_inc(t["cleared"], 1)
        dve.wait_ge(t["loaded"], 32)
        link(dve.tensor_scalar(si, si, NODES - 1, None, ALU.min),
             dve.tensor_scalar(di, di, NO_NODE, None, ALU.min))
        link(dve.tensor_scalar(di, di, ID_BITS, KEY_BASE, ALU.logical_shift_left, ALU.bitwise_or))
        link(dve.tensor_tensor(V[1].bitcast(I32), si, di, ALU.bitwise_or))
        link(dve.tensor_scalar(V[0], V[1], sign(0), None, ALU.mult))

        def compare(a, b, d, flip=False):
            va = a.rearrange("p (n two d) -> p n two d", two=2, d=d)
            vb = b.rearrange("p (n two d) -> p n two d", two=2, d=d)
            lo = va[:, :, 0, :]
            hi = va[:, :, 1, ::-1] if flip else va[:, :, 1, :]
            to = vb[:, :, 1, ::-1] if flip else vb[:, :, 1, :]
            link(dve.tensor_tensor(vb[:, :, 0, :], lo, hi, ALU.min),
                 dve.tensor_tensor(to, lo, hi, ALU.max))

        a, b, c = V[0], V[1], T
        for k in range(1, 11):
            compare(a, b, 1 << (k - 1), True)
            a, b = b, a
            for j in range(k - 2, -1, -1):
                compare(a, b, 1 << j)
                a, b = b, a
            if k == 9 and between:
                between()
        t["swaps"], dmas = [], 0
        for k in range(11, 18):
            link(dve.tensor_scalar(b, a, sign(k - 10), None, ALU.mult))
            a, b = b, a
            for bit in range(k - 11, 4, -1):
                t["swaps"].append((a, b))
                dve.sem_inc(t["swap_asked"], 1)
                link(dve.tensor_scalar(c, a, sign(bit + 3), None, ALU.mult))
                dmas += P >> bit
                dve.wait_ge(t["swapped"], 16 * dmas)
                link(dve.scalar_tensor_tensor(a, b, sign(bit + 3), c, ALU.mult, ALU.min))
                link(dve.tensor_scalar(b, a, sign(bit + 3), None, ALU.mult))
                a, b = b, a
            link(dve.transpose(b, a))
            a, b = b, a
            for j in range(min(k - 11, 4), -1, -1):
                compare(a, b, 1 << j)
                a, b = b, a
            link(dve.transpose(b, a))
            a, b = b, a
            for j in range(9, -1, -1):
                compare(a, b, 1 << j)
                a, b = b, a
        keys = a.bitcast(I32)
        link(dve.tensor_scalar(di, keys, ID_BITS, NO_NODE, ALU.logical_shift_right, ALU.bitwise_and),
             dve.tensor_scalar(si, keys, NO_NODE, None, ALU.bitwise_and))
        link(dve.tensor_copy(t["dst"], di), dve.tensor_copy(t["src"], si))
        dve.sem_inc(t["lists_ready"], 1)

    def lists_sync(sp, t, at_once):
        sp.wait_ge(t["lists_ready"], 1)
        sp.dma_start(t["dst_rows"].rearrange("(p a) b -> p (a b)", p=P), t["dst"]).then_inc(t["dst_stored"], 16)
        sp.wait_ge(zero_filled, 1)
        sp.wait_ge(t["dst_stored"], 16)
        for b in range(ROUNDS):
            if b and b % at_once == 0:
                sp.wait_ge(t["lists_stored"], 16 * b)
            sp.dma_start(bass.AP(t["src_rows"].tensor, ROUNDS + b * (SORTED + ROUNDS - 1), [[F, P], [1, F]]),
                         t["src"]).then_inc(t["lists_stored"], 16)
        sp.dma_start(bass.AP(t["src_rows"].tensor, ROUNDS + SORTED, [[SORTED + ROUNDS - 1, ROUNDS], [1, ROUNDS - 1]]),
                     zero[:, 0:ROUNDS - 1]).then_inc(t["lists_stored"], 16)
        sp.dma_start(t["src_rows"][0:1, :], zero[0:1, :]).then_inc(t["lists_stored"], 16)
        sp.wait_ge(t["lists_stored"], 16 * (ROUNDS + 2))

    def samples_tensor(pe, t):
        pe.wait_ge(t["samples_known"], 1)
        for c in range(t["samples"] // P):
            mm = pe.matmul(t["bc"][:, c * P:(c + 1) * P], ones[:, :], t["diag"][:, c, :], start=True, stop=True)
        mm.then_inc(t["samples_spread"], 1)

    def samples_vector(dve, link, t):
        n, search = t["samples"], t["search"]
        link(*[dve.tensor_scalar(t["diag"][:, c, :], ident, t["dst"][:, c * search:c * search + 1], None, ALU.mult)
               for c in range(n // P)])
        dve.sem_inc(t["samples_known"], 1)
        dve.wait_ge(t["samples_spread"], 1)
        for g in range(SLOTS // 10):
            w0 = g * 10
            for w in range(w0, w0 + 10):
                link(dve.tensor_scalar(t["junk"], t["bc"][:, :], node_id[:, w:w + 1], 0.0,
                                       ALU.is_lt, ALU.add, accum_out=row_f[:, w:w + 1]))
            s = slice(w0, w0 + 10)
            link(dve.tensor_scalar(row_f[:, s], row_f[:, s], -1.0, 0.0, ALU.add, ALU.max))
            link(dve.tensor_copy(row_i[:, s], row_f[:, s]))
            dve.sem_inc(t["rows_known"], 1)

    def search_gpsimd(pool, t):
        pool.wait_ge(t["dst_stored"], 16)
        for w in range(SLOTS):
            if w % 10 == 0:
                pool.wait_ge(t["rows_known"], w // 10 + 1)
            signal = t["rows_got"][w // t["per_signal"]]
            pool.indirect_dma_start(t["rows"][:, w, :], None, t["dst_rows"],
                                    row_index(row_i, w)).then_inc(signal, 16)

    def degrees_vector(dve, link, t):
        search = t["search"]
        for w in range(SLOTS):
            if w % t["per_signal"] == 0:
                dve.wait_ge(t["rows_got"][w // t["per_signal"]], 16 * t["per_signal"])
                counts = []
            counts.append(dve.tensor_scalar(t["rows"][:, w, :], t["rows"][:, w, :], node_id[:, w:w + 1], 0.0,
                                            ALU.is_lt, ALU.add, accum_out=below[:, w:w + 1]))
            if w % t["per_signal"] == t["per_signal"] - 1:
                link(*counts)
        link(dve.scalar_tensor_tensor(first[:, :], row_f[:, :], float(search), below[:, :], ALU.mult, ALU.add))
        link(dve.tensor_tensor(deg[:, :], first[:, 1:SLOTS], first[:, 0:W], ALU.subtract))
        link(dve.memset(ks[0][:, :], BIG_DEGREE))
        link(dve.scalar_tensor_tensor(ks[0][:, 0:W], deg[:, :], 64.0, iota[:, 0:W], ALU.mult, ALU.add))
        a, b = ks
        for k in range(1, 7):
            for j in range(k - 1, -1, -1):
                flip = j == k - 1
                va = a[:, :].rearrange("p (n two d) -> p n two d", two=2, d=1 << j)
                vb = b[:, :].rearrange("p (n two d) -> p n two d", two=2, d=1 << j)
                hi = va[:, :, 1, ::-1] if flip else va[:, :, 1, :]
                to = vb[:, :, 1, ::-1] if flip else vb[:, :, 1, :]
                link(dve.tensor_tensor(vb[:, :, 0, :], va[:, :, 0, :], hi, ALU.min),
                     dve.tensor_tensor(to, va[:, :, 0, :], hi, ALU.max))
                a, b = b, a
        link(dve.tensor_copy(ki[:, :], a[:, :]))
        link(dve.tensor_scalar(ki[:, :], ki[:, :], 63, None, ALU.bitwise_and))
        link(dve.tensor_copy(t["kw"][:, :], ki[:, :]))
        link(dve.tensor_tensor(b[:, :], a[:, :], t["kw"][:, :], ALU.subtract))
        link(dve.tensor_scalar(t["left"][:, :], b[:, 0:W], 1.0 / 64, None, ALU.mult))
        dve.sem_inc(t["cap_ready"], 1)
        hot = t["hot"]
        dve.wait_ge(t["lists_stored"], 16 * (ROUNDS + 2))
        link(dve.tensor_tensor(hot, t["kw"][:, 0:W].unsqueeze(2).to_broadcast([P, W, W]),
                               iota[:, 0:W].unsqueeze(1).to_broadcast([P, W, W]), ALU.is_equal))
        link(dve.tensor_tensor(hot, hot, first[:, 0:W].unsqueeze(1).to_broadcast([P, W, W]), ALU.mult))
        link(dve.tensor_reduce(b[:, 0:W], hot, AX.X, ALU.add))
        link(dve.tensor_copy(ki[:, 0:W], b[:, 0:W]))
        link(dve.tensor_scalar(row_i[:, 0:W], ki[:, 0:W], ROUNDS - 1, None, ALU.bitwise_and),
             dve.tensor_scalar(ki[:, 0:W], ki[:, 0:W], 5, None, ALU.logical_shift_right))
        link(dve.tensor_copy(row_f[:, 0:W], row_i[:, 0:W]), dve.tensor_copy(t["run"][:, :], ki[:, 0:W]))
        link(dve.tensor_scalar(t["copy"][:, :], row_f[:, 0:W], float(SORTED // ROUNDS + 1), 1.0, ALU.mult, ALU.add),
             dve.tensor_scalar(b[:, 0:W], t["kw"][:, 0:W], node_id[:, 0:1], None, ALU.add))
        link(dve.tensor_copy(t["node"][:, :], b[:, 0:W]))

    def dis_vector(dve, link):
        link(dve.tensor_scalar(row_f[:, 0:W], deg[:, :], 1.0, None, ALU.max))
        dve.sem_inc(dis_in, 1)
        dve.wait_ge(dis_root, 1)
        link(dve.reciprocal(ks[1][:, 0:W], below[:, 0:W]))
        link(dve.tensor_scalar(row_f[:, 0:W], deg[:, :], 0.0, None, ALU.is_gt))
        link(dve.tensor_tensor(dis[:, :], ks[1][:, 0:W], row_f[:, 0:W], ALU.mult))
        dve.sem_inc(dis_ok, 1)

    def sources_vector(dve, link, t):
        link(dve.tensor_scalar(prow_f[:, :], t["run"][:, :], float(SORTED // ROUNDS - 1), None, ALU.min))
        link(dve.tensor_tensor(prow_f[:, :], prow_f[:, :], t["copy"][:, :], ALU.add))
        link(dve.tensor_copy(prow_i[:, :], prow_f[:, :]))
        dve.sem_inc(t["src_known"], 1)

    def plan_vector(dve, link, t, per, least):
        dve.wait_ge(t["most_ready"], 1)
        link(dve.tensor_reduce(sc[0][:, 0:1], most[:, :], AX.X, ALU.max))
        link(dve.tensor_scalar(sc[0][:, 0:1], sc[0][:, 0:1], float(ROUNDS - 1), float(ROUNDS), ALU.add, ALU.max))
        link(dve.tensor_copy(nch_i[:, 0:1], sc[0][:, 0:1]))
        link(dve.tensor_scalar(t["passes_i"][:, :], nch_i[:, 0:1], 5, None, ALU.logical_shift_right))
        link(dve.tensor_scalar(most[:, :], most[:, :], float(ROUNDS), float(CHUNK - 1), ALU.min, ALU.add))
        link(dve.tensor_copy(nch_i[:, :], most[:, :]))
        link(dve.tensor_scalar(nch_i[:, :], nch_i[:, :], 2, None, ALU.logical_shift_right))
        link(dve.tensor_copy(nch[:, :], nch_i[:, :]))
        link(dve.tensor_copy(sc[0][:, :], nch[:, :]))
        a, b = sc
        d = 1
        while d < W:
            link(dve.tensor_copy(b[:, 0:d], a[:, 0:d]),
                 dve.tensor_tensor(b[:, d:W], a[:, d:W], a[:, 0:W - d], ALU.add))
            a, b = b, a
            d *= 2
        for c in range(CHUNKS // P):
            link(dve.tensor_scalar(b[:, :], a[:, :], q_id[:, c:c + 1], 0.0, ALU.is_le, ALU.add,
                                   accum_out=slot_f[:, c:c + 1]))
            link(dve.scalar_tensor_tensor(b[:, :], a[:, :], q_id[:, c:c + 1], nch[:, :], ALU.is_le, ALU.mult,
                                          accum_out=off_f[:, c:c + 1]))
        link(dve.tensor_tensor(off_f[:, :], q_id, off_f[:, :], ALU.subtract))
        link(dve.tensor_scalar(off_f[:, :], off_f[:, :], float(CHUNK), None, ALU.mult))
        link(dve.scalar_tensor_tensor(off_f[:, :], slot_f[:, :], float(ROUNDS), off_f[:, :], ALU.mult, ALU.add))
        link(dve.tensor_scalar(off_f[:, :], off_f[:, :], float(W * ROUNDS), None, ALU.min))
        link(dve.tensor_copy(lists_i[:, 0, :], slot_f[:, :]), dve.tensor_copy(lists_i[:, 1, :], off_f[:, :]))
        multiple, under = (flat(t["idx"][:, i * 4:(i + 1) * 4, :]) for i in range(2))
        link(dve.tensor_scalar(multiple, iota, float(per), None, ALU.mult))
        link(dve.tensor_scalar(under, multiple, a[:, W - 1:W], 0.0, ALU.is_lt, ALU.add, accum_out=b[:, 0:1]))
        link(dve.tensor_scalar(b[:, 0:1], b[:, 0:1], float(least), None, ALU.max))
        link(dve.tensor_copy(t["iters_i"][:, :], b[:, 0:1]))
        dve.sem_inc(t["list_ready"], 1)

    def indices_vector(dve, link, t):
        link(dve.tensor_tensor(t["idx"][:, 0:W, :], iota[:, 0:ROUNDS].unsqueeze(1).to_broadcast([P, W, ROUNDS]),
                               t["left"][:, :].unsqueeze(2).to_broadcast([P, W, ROUNDS]), ALU.is_lt))
        dve.wait_ge(t["src_got"], 16 * W)
        link(dve.scalar_tensor_tensor(raw[:, :, :], raw[:, :, :], -float(ZERO_ROW), t["idx"][:, 0:W, :], ALU.add, ALU.mult))
        link(dve.tensor_scalar(t["idx"][:, 0:W, :], raw[:, :, :], float(ZERO_ROW), None, ALU.add),
             dve.memset(t["idx"][:, W:SLOTS, :], float(ZERO_ROW)))
        link(dve.tensor_scalar(t["left"][:, :], t["left"][:, :], -float(ROUNDS), 0.0, ALU.add, ALU.max),
             dve.tensor_scalar(t["run"][:, :], t["run"][:, :], 1.0, None, ALU.add))

    def most_gpsimd(pool, t):
        pool.wait_ge(t["cap_ready"], 1)
        pool.partition_all_reduce(most[:, :], t["left"][:, :], P, REDUCE_MAX).then_inc(t["most_ready"], 1)

    def sources_gpsimd(pool, t, first_pass=True):
        if first_pass:
            pool.wait_ge(t["lists_stored"], 16 * (ROUNDS + 2))
        pool.wait_ge(t["src_known"], 1)
        for w in range(W):
            pool.indirect_dma_start(raw[:, w, :], None, t["src_rows"], row_index(prow_i, w)).then_inc(t["src_got"], 16)

    def plan_sync(sp, t):
        sp.wait_ge(t["list_ready"], 1)
        for h in range(2):
            sp.dma_start(t["lists_d"][h].rearrange("(c p) -> p c", p=P).unsqueeze(2), lists_i[:, h, :].unsqueeze(2),
                         allow_slow_non_contiguous=True).then_inc(t["list_stored"], 16)
        sp.wait_ge(t["list_stored"], 32)
        sp.dma_start(t["lists"][0:1, :], t["lists_d"].rearrange("h q -> (h q)").unsqueeze(0)).then_inc(t["list_loaded"], 16)
        sp.wait_ge(t["list_loaded"], 16)

    PASS_SEMS = ("src_known", "src_got", "cap_ready", "most_ready", "list_ready", "list_stored", "list_loaded",
                 "plan_step")

    def more_passes(t, body_sems, per, body):
        every = [t[n].num for n in PASS_SEMS] + [s.num for v in body_sems.values() for s in (v if isinstance(v, list) else [v])]
        lo, hi = min(every), max(every) + 1
        assert len(every) == hi - lo, "the semaphores of a pass are a block"
        passes = nc.values_load(t["passes_i"][0:1, 0:1], min_val=1, max_val=SORTED // ROUNDS)
        with nc.If(passes > 1):
            with nc.Fori(1, passes):
                nc.all_engine_barrier()
                nc.gpsimd.dma_reset(range(lo, hi))
                nc.gpsimd.sem_clear(range(lo, hi))
                nc.all_engine_barrier()
                with nc.Block() as block:
                    @block.vector
                    def _(dve):
                        link = link_on(dve, t["plan_step"])
                        dve.sem_inc(t["cap_ready"], 1)
                        sources_vector(dve, link, t)
                        plan_vector(dve, link, t, per, 1)
                        indices_vector(dve, link, t)

                    @block.gpsimd
                    def _(pool):
                        most_gpsimd(pool, t)
                        sources_gpsimd(pool, t, False)

                    @block.sync
                    def _(sp):
                        plan_sync(sp, t)
                with nc.Block() as block:
                    body(block)

    def iterations(eng, t, per=RING):
        return eng.value_load(t["iters_i"][0:1, 0:1], min_val=1, max_val=-(-W * ROUNDS // (CHUNK * per)))

    def slot_of(eng, t, it, c, per=RING):
        return eng.value_load(t["lists"][0:1, ds(it * per + c, 1)], min_val=0, max_val=W)

    def stage_indices(act, t, it, c, after, stage, staged, per=RING):
        at = it * per + (CHUNKS + after * per + c)
        off = act.value_load(t["lists"][0:1, ds(at, 1)] if not isinstance(at, int) else t["lists"][0:1, at:at + 1],
                             min_val=0, max_val=W * ROUNDS)
        act.activation(stage[:, c, :], flat(t["idx"][:, :, :])[:, ds(off, CHUNK)], ACT.Copy).then_inc(staged, 1)

    def gather_chunk(pool, it, c, stage, rows, table, free, staged, landed):
        pool.wait_ge(free[c], it + 1)
        pool.wait_ge(staged[c], it + 1)
        pool.nop(nofuse=True)
        for r in range(CHUNK):
            pool.indirect_dma_start(rows[:, c, r, :], None, table, row_index(stage[:, c, :], r)).then_inc(landed[c], 16)

    with top:
        cst = sb("cst", [P, C_END])
        ident = cst[:, C_ID:C_ID + P]
        node_id = cst[:, C_NODE:C_NODE + SLOTS]
        iota = cst[:, C_IOTA:C_IOTA + P]
        q_id = cst[:, C_Q:C_END]

        def sign(k):
            return cst[:, C_SIGN + k:C_SIGN + k + 1]

        X = sb("X", [P, W, D])
        acc = sb("acc", [P, SLOTS, D])
        XT = sb("XT", [P, 2, PADDED])
        dis = sb("dis", [P, W])
        Mx = sb("Mx", [P, 2, D])
        zero, ones = sb("zero", [ROUNDS, ROUNDS]), sb("ones", [P, P])
        raw = sb("raw", [P, W, ROUNDS])
        row_f, row_i = sb("row_f", [P, SLOTS]), sb("row_i", [P, SLOTS], I32)
        below, first, deg = sb("below", [P, SLOTS]), sb("first", [P, SLOTS]), sb("deg", [P, W])
        ks = [sb(f"ks{i}", [P, 64]) for i in range(2)]
        ki = sb("ki", [P, 64], I32)
        most, nch, prow_f = (sb(n, [P, W]) for n in ("most", "nch", "prow_f"))
        sc = [sb(f"sc{i}", [P, W]) for i in range(2)]
        prow_i, nch_i = (sb(n, [P, W], I32) for n in ("prow_i", "nch_i"))
        slot_f, off_f = sb("slot_f", [P, CHUNKS // P]), sb("off_f", [P, CHUNKS // P])
        lists_i = sb("lists_i", [P, 2, CHUNKS // P], I32)

        accf, Xf = flat(acc[:, :, :]), flat(X[:, :, :])
        te = edge_list("e", 256, accf[:, 0:5 * F], accf[:, 0:SLOTS * 256], 10)
        gnn_body = dict(free=[sem(f"g_free{c}") for c in range(RING)], staged=[sem(f"g_staged{c}") for c in range(RING)],
                        landed=[sem(f"g_landed{c}") for c in range(RING)], summed=sem("g_summed"), moved=sem("g_moved"))

        zero_filled, dis_in, dis_root, dis_ok = sems("zero_filled", "dis_in", "dis_root", "dis_ready")

        scope()
        s_in = [sem(f"x_loaded{g}") for g in range(W // GROUP)]
        c_in, x_zero, eps_ok, ln_s, mean_ok, root_ok, rinv_ok, shift_ok, normed, turned, moved, sort_s = sems(
            "consts_loaded", "x_zeroed", "eps_ready", "ln_step", "ln_mean", "ln_root", "ln_rinv", "ln_shift",
            "ln_normed", "ln_turned", "ln_moved", "sort_step")
        ssum, ssq, root, rinv, shift = (sb(n, [P, W]) for n in ("ssum", "ssq", "root", "rinv", "shift"))
        eps = sb("eps", [P, 1])
        sq = sb("sq", [P, D])
        xn = sb("xn", [P, 2, D])
        tp = [pb(f"tp{i}", [P, 2, P]) for i in range(2)]

        def load_gnn(sp, si, di, s):
            n = 125
            sp.dma_start(si[0:n, 0:EDGES_GNN // n], src.rearrange("(p f) -> p f", p=n)).then_inc(s, 16)
            sp.dma_start(di[0:n, 0:EDGES_GNN // n], dst.rearrange("(p f) -> p f", p=n)).then_inc(s, 16)

        def load_x(sp, signals):
            for g in range(W // GROUP):
                s = slice(g * GROUP, (g + 1) * GROUP)
                e = min(LAST, (g + 1) * GROUP)
                sp.dma_start(X[0:FULL, s, :], x[0:FULL * W, :].rearrange("(p w) d -> p w d", w=W)[:, s, :]).then_inc(signals[g], 16)
                if e > g * GROUP:
                    sp.dma_start(X[FULL:P, g * GROUP:e, :],
                                 x[FULL * W + g * GROUP:FULL * W + e, :].unsqueeze(0)).then_inc(signals[g], 16)

        def x_landed(eng, signals, g):
            eng.wait_ge(signals[g], 32 if LAST > g * GROUP else 16)

        with nc.Block() as block:
            @block.vector
            def _(dve):
                link = link_on(dve, sort_s)
                dve.wait_ge(c_in, 16)

                def between():
                    dve.wait_ge(root_ok, 1)
                    link(dve.reciprocal(rinv[:, :], root[:, :]))
                    dve.sem_inc(rinv_ok, 1)
                sort_vector(dve, link, te, between)

            @block.sync
            def _(sp):
                sp.dma_start(cst[:, :], consts).then_inc(c_in, 16)
                sort_sync(sp, te, load_gnn)
                sp.wait_ge(x_zero, 1)
                load_x(sp, s_in)
                swap_sync(sp, te)

            @block.gpsimd
            def _(pool):
                pool.memset(X[96:P, :, :], 0.0).then_inc(x_zero, 1)
                pool.wait_ge(x_zero, 1)
                pool.memset(eps[:, :], EPS).then_inc(eps_ok, 1)
                pool.wait_ge(eps_ok, 1)
                pool.wait_ge(rinv_ok, 1)
                pool.tensor_tensor(shift[:, :], ssum[:, :], rinv[:, :], ALU.mult).then_inc(shift_ok, 1)

            @block.scalar
            def _(act):
                act.wait_ge(x_zero, 1)
                act.wait_ge(eps_ok, 1)
                for g in range(W // GROUP):
                    x_landed(act, s_in, g)
                    for w in range(g * GROUP, (g + 1) * GROUP):
                        if w:
                            act.wait_ge(ln_s, w)
                        act.activation(sq[:, :], X[:, w, :], ACT.Copy, accum_out=ssum[:, w:w + 1]).then_inc(ln_s, 1)
                act.wait_ge(ln_s, W)
                act.mul(ssum[:, :], ssum[:, :], -1.0 / D).then_inc(mean_ok, 1)
                act.wait_ge(mean_ok, 1)
                for w in range(W):
                    act.activation(sq[:, :], X[:, w, :], ACT.Square, bias=ssum[:, w:w + 1],
                                   accum_out=ssq[:, w:w + 1]).then_inc(ln_s, 1)
                    act.wait_ge(ln_s, W + w + 1)
                act.activation(root[:, :], ssq[:, :], ACT.Sqrt, bias=eps[:, 0:1], scale=1.0 / D).then_inc(root_ok, 1)
                act.wait_ge(shift_ok, 1)
                act.wait_ge(rinv_ok, 1)
                for w in range(W + 1):
                    if w < W:
                        if w >= 2:
                            act.wait_ge(turned, w - 1)
                        act.activation(xn[:, w % 2, :], X[:, w, :], ACT.Identity,
                                       bias=shift[:, w:w + 1], scale=rinv[:, w:w + 1]).then_inc(normed, 1)
                    if w:
                        act.wait_ge(turned, w)
                        act.activation(XT[:, :, (w - 1) * P:w * P], tp[(w - 1) % 2][:, :, :], ACT.Copy).then_inc(moved, 1)

            @block.tensor
            def _(pe):
                pe.wait_ge(c_in, 16)
                for w in range(W):
                    pe.wait_ge(normed, w + 1)
                    if w >= 2:
                        pe.wait_ge(moved, w - 1)
                    for c in range(2):
                        mm = pe.transpose(tp[w % 2][:, c, :], xn[:, w % 2, c * P:(c + 1) * P], ident)
                    mm.then_inc(turned, 1)
        leave()
        if debug and debug[0] == "xt":
            return debug[1](nc, sem, out, XT)

        scope()
        te["rows"] = flat(X[:, :, :])[:, 0:W * D].rearrange("p (s k) -> p s k", k=256)
        spare = sb("spare_rows", [P, 256])
        te["rows_last"] = spare
        te["diag"] = sb("diag", [P, 4, P])
        te["junk"] = sb("junk", [P, 512])[:, :]
        te["bc"] = pb("bc", [P, 512])
        te["hot"] = accf[:, 5 * F:5 * F + W * W].rearrange("p (a b) -> p a b", b=W)
        gw = sb("gw", [P, 2, D])
        hb = [sb(f"hb{i}", [P, GROUP, D]) for i in range(2)]
        zrow = sb("zrow", [1, D])
        hp = [pb(f"hp{i}", [P, D]) for i in range(2)]
        gw_in, h_mm, h_ok, z_ok, step2, acc0 = sems("gw_loaded", "h_product", "h_scaled", "zero_row", "degree_step", "acc_zeroed")
        h_out = [sem(f"h_stored{i}") for i in range(2)]

        class Rows:
            def __getitem__(self, key):
                _, w, cols = key
                return te["x_rows"][:, w, cols] if w < W else te["rows_last"][:, cols]
        te["x_rows"], te["rows"] = te["rows"], Rows()
        with nc.Block() as block:
            @block.sync
            def _(sp):
                for c in range(2):
                    sp.dma_start(gw[:, c, :], gnn_w[c * P:(c + 1) * P, :]).then_inc(gw_in, 16)
                lists_sync(sp, te, 4)
                plan_sync(sp, te)
                sp.wait_ge(z_ok, 1)
                sp.dma_start(tab_gnn[ZERO_ROW:ZERO_ROW + 1, :], zrow[:, :]).then_inc(gw_in, 16)
                sp.wait_ge(gw_in, 48)

            @block.gpsimd
            def _(pool):
                search_gpsimd(pool, te)
                most_gpsimd(pool, te)
                sources_gpsimd(pool, te)
                pool.wait_ge(acc0, 1)

            @block.vector
            def _(dve):
                link = link_on(dve, step2)
                link(dve.memset(zrow[:, :], 0.0), dve.memset(zero[:, :], 0.0), dve.memset(ones[:, :], 1.0))
                dve.sem_inc(z_ok, 1)
                dve.sem_inc(zero_filled, 1)
                samples_vector(dve, link, te)
                degrees_vector(dve, link, te)
                sources_vector(dve, link, te)
                dis_vector(dve, link)
                plan_vector(dve, link, te, RING, MIX_END + 1)
                link(dve.memset(accf[:, :], 0.0))
                dve.sem_inc(acc0, 1)
                indices_vector(dve, link, te)

            @block.tensor
            def _(pe):
                samples_tensor(pe, te)
                pe.wait_ge(gw_in, 32)
                for w in range(W):
                    if w >= 2:
                        pe.wait_ge(h_ok, w - 1)
                    for c in range(2):
                        mm = pe.matmul(hp[w % 2][:, :], XT[:, c, w * P:(w + 1) * P], gw[:, c, :], start=(c == 0), stop=(c == 1))
                    mm.then_inc(h_mm, 1)

            @block.scalar
            def _(act):
                act.wait_ge(dis_in, 1)
                act.activation(below[:, 0:W], row_f[:, 0:W], ACT.Sqrt).then_inc(dis_root, 1)
                act.wait_ge(dis_ok, 1)
                tv = tab_gnn[0:PADDED, :].rearrange("(p w) d -> p w d", w=W)
                for w in range(W):
                    g, b = w // GROUP, w // GROUP % 2
                    if w % GROUP == 0 and g >= 2:
                        act.wait_ge(h_out[b], 16 * (g // 2))
                    act.wait_ge(h_mm, w + 1)
                    act.activation(hb[b][:, w % GROUP, :], hp[w % 2][:, :], ACT.Copy, scale=dis[:, w:w + 1]).then_inc(h_ok, 1)
                    if w % GROUP == GROUP - 1:
                        act.wait_ge(h_ok, w + 1)
                        act.dma_start(tv[:, g * GROUP:(g + 1) * GROUP, :], hb[b][:, :, :]).then_inc(h_out[b], 16)
                for b in range(2):
                    act.wait_ge(h_out[b], 16 * ((W // GROUP + 1 - b) // 2))
        leave()
        if debug and debug[0] == "deg":
            return debug[1](nc, sem, out, dis, te["left"], te["node"])

        ta = edge_list("a", 128, Xf[:, 0:5 * F], Xf[:, 5 * F:5 * F + SLOTS * 128], SLOTS)
        ta["diag"] = Xf[:, 5 * F:5 * F + 8 * P].rearrange("p (c q) -> p c q", q=P)
        ta["junk"] = Xf[:, 3 * F:4 * F]
        ta["hot"] = Xf[:, 0:W * W].rearrange("p (a b) -> p a b", b=W)
        gat_body = dict(free=[sem(f"a_free{h}") for h in range(2)], staged=[sem(f"a_staged{h}") for h in range(2)],
                        landed=[sem(f"a_landed{q}") for q in range(GAT_RING)], step=sem("a_step"),
                        exp_in=sem("a_exp_in"), exp_out=sem("a_exp_out"))
        scope()
        rows = sb("rows", [P, RING, CHUNK, D])
        stage = sb("stage", [P, RING, CHUNK], I32)
        sp_ps = [pb(f"sum_ps{i}", [P, D]) for i in range(2)]
        free, staged, landed, summed, moved = (gnn_body[n] for n in ("free", "staged", "landed", "summed", "moved"))

        def load_gat(sp, si, di, s):
            sp.dma_start(si, gat_edges[0].rearrange("(p f) -> p f", p=P)).then_inc(s, 16)
            sp.dma_start(di, gat_edges[1].rearrange("(p f) -> p f", p=P)).then_inc(s, 16)

        def sum_chunk(pe, it, c):
            n = it * RING + c
            at = slot_of(pe, te, it, c)
            pe.wait_ge(landed[c], (it + 1) * (16 * CHUNK))
            pe.wait_ge(moved, n + 1)
            for r in range(CHUNK):
                mm = pe.matmul(sp_ps[c % 2][:, :], ident, rows[:, c, r, :], start=(r == 0), stop=False)
            mm.then_inc(free[c], 1)
            pe.wait_ge(moved, n + 2)
            pe.matmul(sp_ps[c % 2][:, :], ident, flat(acc[:, ds(at, 1), :]), start=False, stop=True).then_inc(summed, 1)

        def move_chunk(act, it, c, next_too=True):
            at = slot_of(act, te, it, c)
            act.wait_ge(summed, it * RING + (c + 1))
            act.activation(flat(acc[:, ds(at, 1), :]), sp_ps[c % 2][:, :], ACT.Copy).then_inc(moved, 1)
            stage_indices(act, te, it, c, 1, stage, staged[c])

        def sum_begin(act):
            act.sem_inc(moved, 2)
            for c in range(RING):
                stage_indices(act, te, 0, c, 0, stage, staged[c])

        def sum_free(pe):
            for c in range(RING):
                pe.sem_inc(free[c], 1)

        def sum_body(block):
            @block.scalar
            def _(act):
                sum_begin(act)
                with act.Fori(0, iterations(act, te)) as it:
                    for c in range(RING):
                        move_chunk(act, it, c)

            @block.gpsimd
            def _(pool):
                with pool.Fori(0, iterations(pool, te)) as it:
                    for c in range(RING):
                        gather_chunk(pool, it, c, stage, rows, tab_gnn, free, staged, landed)

            @block.tensor
            def _(pe):
                sum_free(pe)
                with pe.Fori(0, iterations(pe, te)) as it:
                    for c in range(RING):
                        sum_chunk(pe, it, c)

        scope()
        at = [0]

        def in_x(*shape):
            n = 1
            for d in shape:
                n *= d
            at[0] += n
            ap = Xf[:, at[0] - n:at[0]]
            return ap if len(shape) == 1 else ap.rearrange("p (a b) -> p a b", a=shape[0])

        wkv = in_x(2, 2 * D)
        gkv, bkv, wmean = in_x(2 * D), in_x(2 * D), in_x(16)
        xw = in_x(3, 2 * P)
        kv, sq = in_x(3, 2 * D), in_x(3, 2 * D)
        ssq, rt, rv = in_x(3, 8), in_x(3, 8), in_x(3, 8)
        wq_sb, wo_sb, bd, bw = in_x(2, D), in_x(2, D), in_x(2, P), in_x(2, D)
        kvp = [pb(f"kvp{i}", [P, 2 * D]) for i in range(3)]
        kvs = pb("kvs", [P, 2, 512])
        ta["bc"] = flat(kvs[:, :, :])
        (x_freed, w_in, mix_s, centred, xw_ok, product, squared, var_ok, root_ok, kv_ok, kv_used, bd_ok, bw_mm, bw_ok,
         m_mm, mid) = sems(
            "x_freed", "mix_loaded", "list2_step", "kv_centred", "xw_ready", "kv_product", "kv_squared", "kv_var",
            "kv_root", "kv_ready", "kv_used", "bd_ready", "bw_product", "bw_ready", "m_product", "mix_step")

        with nc.Block() as block:
            @block.vector
            def _(dve):
                link = link_on(dve, mix_s)
                sort_vector(dve, link, ta)
                samples_vector(dve, link, ta)
                degrees_vector(dve, link, ta)
                sources_vector(dve, link, ta)
                plan_vector(dve, link, ta, GAT_RING, PAIRS + 1)
                indices_vector(dve, link, ta)
                link(dve.memset(bd, 0.0))
                dve.sem_inc(x_freed, 1)
                dve.wait_ge(w_in, 160)
                g = wkv.rearrange("p c (h e) -> p (c h) e", e=HEAD_DIM)
                link(dve.tensor_reduce(wmean, g, AX.X, ALU.add))
                link(dve.tensor_scalar(wmean, wmean, 1.0 / HEAD_DIM, None, ALU.mult))
                link(dve.tensor_tensor(g, g, wmean.unsqueeze(2).to_broadcast([P, 16, HEAD_DIM]), ALU.subtract))
                dve.sem_inc(centred, 1)
                STEPS = 4

                def heads(a):
                    return a.rearrange("p (h e) -> p h e", e=HEAD_DIM)

                def normalize(w, b):
                    k = w * STEPS
                    dve.wait_ge(squared, w + 1)
                    dve.tensor_reduce(ssq[:, b, :], heads(sq[:, b, :]), AX.X, ALU.add).then_inc(mid, 1)
                    dve.wait_ge(mid, k + 1)
                    dve.tensor_scalar(ssq[:, b, :], ssq[:, b, :], 1.0 / HEAD_DIM, EPS, ALU.mult, ALU.add).then_inc(var_ok, 1)
                    dve.wait_ge(root_ok, w + 1)
                    dve.reciprocal(rv[:, b, :], rt[:, b, :]).then_inc(mid, 1)
                    dve.wait_ge(mid, k + 2)
                    if not (isinstance(w, int) and w < 3):
                        dve.wait_ge(kv_used, w - 2)
                    dve.tensor_tensor(heads(kv[:, b, :]), heads(kvp[b][:, :]),
                                      rv[:, b, :].unsqueeze(2).to_broadcast([P, 8, HEAD_DIM]), ALU.mult).then_inc(mid, 1)
                    dve.wait_ge(mid, k + 3)
                    dve.tensor_tensor(kv[:, b, :], kv[:, b, :], gkv, ALU.mult).then_inc(mid, 1)
                    dve.wait_ge(mid, k + 4)
                    dve.tensor_tensor(kv[:, b, :], kv[:, b, :], bkv, ALU.add).then_inc(kv_ok, 1)

                normalize(0, 0)
                for j in range(3):
                    normalize(j + 1, (j + 1) % 3)
                with dve.Fori(1, MIX_STEPS) as i:
                    for j in range(3):
                        normalize(i * 3 + (j + 1), (j + 1) % 3)
                dve.wait_ge(kv_used, W)
                for q in range(2):
                    for h in range(2):
                        s = slice(h * 64, h * 64 + 64)
                        dve.tensor_scalar(bd[s, q, s], kvs[s, q, s], 1.0 / NODES, None, ALU.mult).then_inc(bd_ok, 1)
                dve.wait_ge(bw_mm, 1)
                dve.tensor_copy(bw, kvs[:, :, 0:D]).then_inc(bw_ok, 1)
                dve.wait_ge(m_mm, 1)
                dve.tensor_copy(Mx[:, :, :], kvs[:, :, D:2 * D])

            @block.sync
            def _(sp):
                sort_sync(sp, ta, load_gat)
                swap_sync(sp, ta)
                lists_sync(sp, ta, 2)
                plan_sync(sp, ta)
                sp.wait_ge(x_freed, 1)
                for c in range(2):
                    sp.dma_start(wkv[:, c, 0:D], wk_t[c * P:(c + 1) * P, :]).then_inc(w_in, 16)
                    sp.dma_start(wkv[:, c, D:2 * D], wv_t[c * P:(c + 1) * P, :]).then_inc(w_in, 16)
                    sp.dma_start(wq_sb[:, c, :], wq[c * P:(c + 1) * P, :]).then_inc(w_in, 16)
                    sp.dma_start(wo_sb[:, c, :], wo_t[c * P:(c + 1) * P, :]).then_inc(w_in, 16)
                sp.dma_start(gkv, lnkv[0:1, :].to_broadcast([P, 2 * D])).then_inc(w_in, 16)
                sp.dma_start(bkv, lnkv[1:2, :].to_broadcast([P, 2 * D])).then_inc(w_in, 16)

            @block.gpsimd
            def _(pool):
                n = iterations(pool, te)
                for i0, i1, then in ((0, SEARCH_IT, (search_gpsimd,)), (SEARCH_IT, SOURCES_IT, (sources_gpsimd, most_gpsimd)),
                                     (SOURCES_IT, n, ())):
                    with pool.Fori(i0, i1) as it:
                        for c in range(RING):
                            gather_chunk(pool, it, c, stage, rows, tab_gnn, free, staged, landed)
                    for step in then:
                        step(pool, ta)

            @block.scalar
            def _(act):
                n = iterations(act, te)

                def copy_window(w, b):
                    if not (isinstance(w, int) and w < 3):
                        act.wait_ge(product, w - 2)
                    act.activation(xw[:, b, :].rearrange("p (c q) -> p c q", c=2), XT[:, :, ds(w * P, P)],
                                   ACT.Copy).then_inc(xw_ok, 1)

                def square(w, b):
                    act.wait_ge(product, w + 1)
                    act.activation(sq[:, b, :], kvp[b][:, :], ACT.Square).then_inc(squared, 1)

                def take_root(w, b):
                    act.wait_ge(var_ok, w + 1)
                    act.activation(rt[:, b, :], ssq[:, b, :], ACT.Sqrt).then_inc(root_ok, 1)

                def mix_step(it, w0):
                    b = (1, 2, 0)
                    w = [w0 + j for j in range(3)]
                    for j in range(3):
                        copy_window(w[j], b[j])
                    after = {0: (square, 0), 1: (take_root, 0), 3: (square, 1), 4: (take_root, 1), 6: (square, 2),
                             7: (take_root, 2)}
                    for q in range(2 * RING):
                        move_chunk(act, it + q // RING, q % RING)
                        if q in after:
                            act_on, j = after[q]
                            act_on(w[j], b[j])

                sum_begin(act)
                with act.Fori(0, MIX_IT) as it:
                    for c in range(RING):
                        move_chunk(act, it, c)
                act.wait_ge(x_freed, 1)
                copy_window(0, 0)
                square(0, 0)
                take_root(0, 0)
                mix_step(MIX_IT, 1)
                with act.Fori(1, MIX_STEPS) as i:
                    mix_step(i * 2 + MIX_IT, i * 3 + 1)
                with act.Fori(MIX_END, n) as it:
                    for c in range(RING):
                        move_chunk(act, it, c)

            @block.tensor
            def _(pe):
                n = iterations(pe, te)

                def product_of(w, b):
                    pe.wait_ge(xw_ok, w + 1)
                    if not (isinstance(w, int) and w < 3):
                        pe.wait_ge(kv_ok, w - 2)
                    for c in range(2):
                        mm = pe.matmul(kvp[b][:, :], xw[:, b, c * P:(c + 1) * P], wkv[:, c, :], start=(c == 0), stop=(c == 1))
                    mm.then_inc(product, 1)

                def sum_kv(w, b, count, first=False):
                    pe.wait_ge(kv_ok, w + 1)
                    for q in range(2):
                        mm = pe.matmul(kvs[:, q, 0:P], kv[0:count, b, D + q * P:D + (q + 1) * P],
                                       kv[0:count, b, q * P:(q + 1) * P], start=first, stop=False, skip_group_check=True)
                    mm.then_inc(kv_used, 1)

                def mix_step(it, w0, counts):
                    b = (1, 2, 0)
                    w = [w0 + j for j in range(3)]
                    product_of(w[0], b[0])
                    for q in range(2 * RING):
                        sum_chunk(pe, it + q // RING, q % RING)
                        if q in (2, 5):
                            j = q // 3
                            sum_kv(w[j], b[j], counts[j])
                            product_of(w[j + 1], b[j + 1])
                    sum_kv(w[2], b[2], counts[2])

                sum_free(pe)
                with pe.Fori(0, SEARCH_IT - 4) as it:
                    for c in range(RING):
                        sum_chunk(pe, it, c)
                samples_tensor(pe, ta)
                with pe.Fori(SEARCH_IT - 4, MIX_IT) as it:
                    for c in range(RING):
                        sum_chunk(pe, it, c)
                pe.wait_ge(centred, 1)
                product_of(0, 0)
                sum_kv(0, 0, P, first=True)
                full = (LAST - 1) // 3
                mix_step(MIX_IT, 1, (P, P, P))
                with pe.Fori(1, full) as i:
                    mix_step(i * 2 + MIX_IT, i * 3 + 1, (P, P, P))
                mix_step(full * 2 + MIX_IT, full * 3 + 1, [P if full * 3 + 1 + j < LAST else FULL for j in range(3)])
                with pe.Fori(full + 1, MIX_STEPS) as i:
                    mix_step(i * 2 + MIX_IT, i * 3 + 1, (FULL, FULL, FULL))
                pe.wait_ge(bd_ok, 4)
                for q in range(2):
                    mm = pe.matmul(kvs[:, q, 0:D], bd[:, q, :], wo_sb[:, q, :], start=True, stop=True)
                mm.then_inc(bw_mm, 1)
                pe.wait_ge(bw_ok, 1)
                for i in range(2):
                    for q in range(2):
                        mm = pe.matmul(kvs[:, i, D:2 * D], wq_sb[:, q, i * P:(i + 1) * P], bw[:, q, :],
                                       start=(q == 0), stop=(q == 1))
                mm.then_inc(m_mm, 1)
                with pe.Fori(MIX_END, n) as it:
                    for c in range(RING):
                        sum_chunk(pe, it, c)
        leave()
        more_passes(te, gnn_body, RING, sum_body)
        leave()
        if debug and debug[0] == "b3":
            return debug[1](nc, sem, out, acc, Mx, te["node"])

        scope()
        own = flat(te["idx"][:, :, :])[:, 0:SLOTS * GATW].rearrange("p (s c) -> p s c", c=GATW)
        state = sb("state", [P, SLOTS, GATV])
        top_score = sb("top_score", [P, SLOTS, HEADS])
        scope()
        bo_sb = sb("bo_sb", [P, D])
        stats, mv = sb("stats", [P, W, 6]), sb("mv", [P, W, 2])
        var, root, rinv, shift = (sb(n + "2", [P, W]) for n in ("var", "root", "rinv", "shift"))
        xn = sb("xn2", [P, 3, D])
        wg, att_sb = sb("wg", [P, 2, 16]), sb("att_sb", [P, 2, 16])
        tab = sb("tab", [P, W, GATW])
        prod = flat(raw[:, :, :])[:, 0:W * 16].rearrange("p (w c) -> p w c", c=16)
        zrow = sb("zrow2", [1, GATW])
        mp = [pb(f"mp{i}", [P, D]) for i in range(2)]
        tp = [pb(f"tp2{i}", [P, 2, P]) for i in range(3)]
        hp = pb("hp16", [P, 1024])
        agg_in = [sem(f"agg_loaded{i}") for i in range((W // GROUP + 1) // 2)]
        (w_in, x_free, scattered, xm, x_pre, deg_s, var_ok, root_ok, rinv_ok, normed, turned, moved,
         h16, tab_ok, tab_out, own_in) = sems(
            "gap_loaded", "x_free", "agg_scattered", "xm_product", "x_added", "gap_step",
            "ln2_var", "ln2_root", "ln2_rinv", "ln2_normed", "ln2_turned", "ln2_moved", "h16_product", "tab_ready",
            "tab_stored", "own_rows")
        groups = W // GROUP
        AHEAD = 7

        with nc.Block() as block:
            @block.gpsimd
            def _(pool):
                for w in range(W):
                    pool.indirect_dma_start(agg_gnn, row_index(te["node"], w), acc[:, w, :], None).then_inc(scattered, 16)
                pool.wait_ge(tab_out, 32)
                for w in range(W):
                    pool.indirect_dma_start(own[:, w, :], None, tab_gat, row_index(ta["node"], w)).then_inc(own_in, 16)

            @block.vector
            def _(dve):
                link = link_on(dve, deg_s)
                dve.memset(X[96:P, LAST:W, :], 0.0).then_inc(x_free, 1)
                link(dve.memset(tab[:, :, :], 1.0), dve.memset(zrow[:, :], 0.0), dve.memset(own[:, W:SLOTS, :], 0.0))
                link(dve.memset(zrow[:, GATV:GATV + HEADS], -1e30))

                def scales(g):
                    s = slice(g * GROUP, (g + 1) * GROUP)
                    dve.wait_ge(root_ok, g + 1)
                    link(dve.reciprocal(rinv[:, s], root[:, s]))
                    link(dve.scalar_tensor_tensor(shift[:, s], mv[:, s, 0], -1.0, rinv[:, s], ALU.mult, ALU.mult))
                    dve.sem_inc(rinv_ok, 1)

                def add_xm(g):
                    dve.wait_ge(s_in[g], 2 * (32 if LAST > g * GROUP else 16))
                    for w in range(g * GROUP, (g + 1) * GROUP):
                        dve.wait_ge(xm, w + 1)
                        dve.tensor_tensor(X[:, w, :], X[:, w, :], mp[w % 2][:, :], ALU.add).then_inc(x_pre, 1)
                    dve.wait_ge(x_pre, (g + 1) * GROUP)
                    s = slice(g * GROUP, (g + 1) * GROUP)
                    link(dve.tensor_tensor(X[:, s, :], X[:, s, :],
                                           bo_sb[:, :].unsqueeze(1).to_broadcast([P, GROUP, D]), ALU.add))

                def add_sums(g):
                    s, ws = slice(g * GROUP, (g + 1) * GROUP), range(g * GROUP, (g + 1) * GROUP)
                    dve.wait_ge(agg_in[g // 2], 16 * min(2, groups - g // 2 * 2))
                    link(*[dve.scalar_tensor_tensor(X[:, w, :], acc[:, w, :], dis[:, w:w + 1], X[:, w, :],
                                                    ALU.mult, ALU.add) for w in ws])
                    link(*[dve.bn_stats(stats[:, w, :], X[:, w, :]) for w in ws])
                    link(*[dve.bn_aggr(mv[:, w, :], stats[:, w, :]) for w in ws])
                    link(dve.tensor_scalar(var[:, s], mv[:, s, 1], EPS, None, ALU.add))
                    dve.sem_inc(var_ok, 1)

                dve.wait_ge(w_in, 16 * 5)
                for g in range(AHEAD):
                    add_xm(g)
                for g in range(groups):
                    if g + AHEAD < groups:
                        add_xm(g + AHEAD)
                    add_sums(g)
                    if g:
                        scales(g - 1)
                scales(groups - 1)
                dve.wait_ge(h16, 1)
                hv = hp[:, 0:W * 16].rearrange("p (w c) -> p w c", c=16)
                to = tab[:, :, 0:GATV].rearrange("p w (h e) -> p w h e", h=HEADS)[:, :, :, 0:EXPERTS]
                link(dve.tensor_copy(to, hv.rearrange("p w (h e) -> p w h e", h=HEADS)))
                for c in range(2):
                    link(dve.tensor_tensor(prod[:, :, :], hv, att_sb[:, c, :].unsqueeze(1).to_broadcast([P, W, 16]), ALU.mult))
                    link(dve.tensor_reduce(tab[:, :, GATV + c * HEADS:GATV + (c + 1) * HEADS],
                                           prod[:, :, :].rearrange("p w (h e) -> p w h e", h=HEADS), AX.X, ALU.add))
                dve.sem_inc(tab_ok, 1)
                dve.wait_ge(own_in, 16 * W)
                link(dve.tensor_copy(state[:, :, :], own[:, :, 0:GATV]),
                     dve.tensor_tensor(top_score[:, :, :], own[:, :, GATV:GATV + HEADS], own[:, :, GATV + HEADS:GATW], ALU.add))
                link(dve.scalar_tensor_tensor(top_score[:, :, :], top_score[:, :, :], 0.2, top_score[:, :, :], ALU.mult, ALU.max))

            @block.sync
            def _(sp):
                sp.dma_start(bo_sb[:, :], bo.unsqueeze(0).to_broadcast([P, D])).then_inc(w_in, 16)
                for c in range(2):
                    sp.dma_start(wg[:, c, :], gat_w[c * P:(c + 1) * P, :]).then_inc(w_in, 16)
                    sp.dma_start(att_sb[:, c, :], att[c:c + 1, :].to_broadcast([P, 16])).then_inc(w_in, 16)
                sp.wait_ge(x_free, 1)
                load_x(sp, s_in)
                sp.wait_ge(scattered, 16 * W)
                av = agg_gnn.rearrange("(p w) d -> p w d", w=W)
                for g in range(groups):
                    s = slice(g * GROUP, (g + 1) * GROUP)
                    sp.dma_start(acc[:, s, :], av[:, s, :]).then_inc(agg_in[g // 2], 16)
                sp.wait_ge(tab_ok, 1)
                sp.dma_start(tab_gat[0:PADDED, :].rearrange("(p w) c -> p w c", w=W), tab[:, :, :]).then_inc(tab_out, 16)
                sp.dma_start(tab_gat[ZERO_ROW:ZERO_ROW + 1, :], zrow[:, :]).then_inc(tab_out, 16)
                sp.wait_ge(tab_out, 32)

            @block.tensor
            def _(pe):
                pe.wait_ge(w_in, 16 * 5)

                def h16_of(w):
                    pe.wait_ge(moved, w + 1)
                    for c in range(2):
                        mm = pe.matmul(hp[:, w * 16:(w + 1) * 16], XT[:, c, w * P:(w + 1) * P], wg[:, c, :],
                                       start=(c == 0), stop=(c == 1))
                    return mm

                behind = AHEAD + 1
                for g in range(groups + behind):
                    if g < groups:
                        for w in range(g * GROUP, (g + 1) * GROUP):
                            if w >= 2:
                                pe.wait_ge(x_pre, w - 1)
                            for c in range(2):
                                mm = pe.matmul(mp[w % 2][:, :], XT[:, c, w * P:(w + 1) * P], Mx[:, c, :], start=(c == 0), stop=(c == 1))
                            mm.then_inc(xm, 1)
                    if g >= behind:
                        for w in range((g - behind) * GROUP, (g - behind + 1) * GROUP):
                            pe.wait_ge(normed, w + 1)
                            if w >= 3:
                                pe.wait_ge(moved, w - 2)
                            for c in range(2):
                                mm = pe.transpose(tp[w % 3][:, c, :], xn[:, w % 3, c * P:(c + 1) * P], ident)
                            mm.then_inc(turned, 1)
                            if w >= 3:
                                h16_of(w - 3)
                h16_of(W - 3)
                h16_of(W - 2)
                h16_of(W - 1).then_inc(h16, 1)

            @block.scalar
            def _(act):
                def move(w):
                    act.wait_ge(turned, w + 1)
                    act.wait_ge(xm, w + 1)
                    act.activation(XT[:, :, w * P:(w + 1) * P], tp[w % 3][:, :, :], ACT.Copy).then_inc(moved, 1)

                for g in range(groups + 1):
                    if g < groups:
                        s = slice(g * GROUP, (g + 1) * GROUP)
                        act.wait_ge(var_ok, g + 1)
                        act.activation(root[:, s], var[:, s], ACT.Sqrt).then_inc(root_ok, 1)
                    if g:
                        act.wait_ge(rinv_ok, g)
                        for w in range((g - 1) * GROUP, g * GROUP):
                            if w >= 3:
                                act.wait_ge(turned, w - 2)
                            act.activation(xn[:, w % 3, :], X[:, w, :], ACT.Identity,
                                           bias=shift[:, w:w + 1], scale=rinv[:, w:w + 1]).then_inc(normed, 1)
                            if w >= 2:
                                move(w - 2)
                move(W - 2)
                move(W - 1)
        leave()
        if debug and debug[0] == "gap":
            debug[1](nc, sem, out, X, XT, ta["left"], ta["node"], state)
            leave()
            return

        HALF = GAT_RING // 2
        scope()
        rows = sb("a_rows", [P, GAT_RING, CHUNK, GATW])
        stage = sb("a_stage", [P, GAT_RING, CHUNK], I32)
        e = sb("a_e", [P, GAT_RING, CHUNK + 1, HEADS])
        high, top_of = (sb(n, [P, GAT_RING, HEADS]) for n in ("a_high", "a_top"))
        pr, part = sb("a_pr", [P, HALF, CHUNK, GATV]), sb("a_part", [P, HALF, GATV])
        free, staged, landed, step, exp_in, exp_out = (gat_body[n] for n in
                                                       ("free", "staged", "landed", "step", "exp_in", "exp_out"))
        PER_HALF = 7 * HALF + 4

        def gather_half(pool, it, h):
            pool.wait_ge(free[h], it + 1)
            pool.wait_ge(staged[h], it * HALF + HALF)
            pool.nop(nofuse=True)
            for q in range(h * HALF, (h + 1) * HALF):
                for r in range(CHUNK):
                    pool.indirect_dma_start(rows[:, q, r, :], None, tab_gat,
                                            row_index(stage[:, q, :], r)).then_inc(landed[q], 16)

        def exp_half(act, it, h):
            qs = slice(h * HALF, (h + 1) * HALF)
            act.wait_ge(exp_in, it * 2 + (h + 1))
            act.activation(e[:, qs, :, :], e[:, qs, :, :], ACT.Exp).then_inc(exp_out, 1)
            for q in range(h * HALF, (h + 1) * HALF):
                stage_indices(act, ta, it, q, 1, stage, staged[h], GAT_RING)

        def attend_half(dve, it, h):
            n = [0]

            def link(*steps):
                for s in steps:
                    s.then_inc(step, 1)
                    n[0] += 1
                dve.wait_ge(step, it * (2 * PER_HALF) + (h * PER_HALF + n[0]))

            q0 = h * HALF
            qs = slice(q0, q0 + HALF)
            at = [slot_of(dve, ta, it, q, GAT_RING) for q in range(q0, q0 + HALF)]
            for q in range(q0, q0 + HALF):
                dve.wait_ge(landed[q], it * (16 * CHUNK) + 16 * CHUNK)
                dve.tensor_tensor(e[:, q, 0:CHUNK, :], rows[:, q, :, GATV:GATV + HEADS],
                                  own[:, ds(at[q - q0], 1), GATV + HEADS:GATW].to_broadcast([P, CHUNK, HEADS]),
                                  ALU.add).then_inc(step, 1)
                n[0] += 1
            dve.wait_ge(step, it * (2 * PER_HALF) + (h * PER_HALF + n[0]))
            link(dve.scalar_tensor_tensor(e[:, qs, 0:CHUNK, :], e[:, qs, 0:CHUNK, :], 0.2, e[:, qs, 0:CHUNK, :],
                                          ALU.mult, ALU.max))
            link(dve.tensor_reduce(high[:, qs, :], e[:, qs, 0:CHUNK, :].rearrange("p q r h -> p q h r"), AX.X, ALU.max))
            for q in range(q0, q0 + HALF):
                m = flat(top_score[:, ds(at[q - q0], 1), :])
                link(dve.tensor_tensor(e[:, q, CHUNK, :], m, m, ALU.max), dve.tensor_tensor(top_of[:, q, :], high[:, q, :], m, ALU.max))
                link(dve.tensor_tensor(m, top_of[:, q, :], top_of[:, q, :], ALU.max))
            link(dve.tensor_tensor(e[:, qs, :, :], e[:, qs, :, :],
                                   top_of[:, qs, :].unsqueeze(2).to_broadcast([P, HALF, CHUNK + 1, HEADS]), ALU.subtract))
            dve.sem_inc(exp_in, 1)
            dve.wait_ge(exp_out, it * 2 + (h + 1))
            for c in range(HALF):
                link(dve.tensor_tensor(pr[:, c, :, :].rearrange("p r (h v) -> p r h v", h=HEADS),
                                       rows[:, q0 + c, :, 0:GATV].rearrange("p r (h v) -> p r h v", h=HEADS),
                                       e[:, q0 + c, 0:CHUNK, :].unsqueeze(3).to_broadcast([P, CHUNK, HEADS, EXPERTS + 1]),
                                       ALU.mult))
            dve.sem_inc(free[h], 1)
            link(dve.tensor_reduce(part[:, :, :], pr[:, :, :, :].rearrange("p c r v -> p c v r"), AX.X, ALU.add))
            for c in range(HALF):
                my = state[:, ds(at[c], 1), :].rearrange("p s (h v) -> p (s h) v", h=HEADS)
                link(dve.tensor_tensor(my, my, e[:, q0 + c, CHUNK, :].unsqueeze(2).to_broadcast([P, HEADS, EXPERTS + 1]), ALU.mult))
                link(dve.tensor_tensor(my, my, part[:, c, :].rearrange("p (h v) -> p h v", h=HEADS), ALU.add))
            assert n[0] == PER_HALF, n[0]

        def attend_free(dve):
            for h in range(2):
                dve.sem_inc(free[h], 1)

        def stage_first(act):
            for q in range(GAT_RING):
                stage_indices(act, ta, 0, q, 0, stage, staged[q // HALF], GAT_RING)

        def gather_all(pool):
            with pool.Fori(0, iterations(pool, ta, GAT_RING)) as it:
                for h in range(2):
                    gather_half(pool, it, h)

        def gat_pass(block):
            @block.scalar
            def _(act):
                stage_first(act)
                with act.Fori(0, iterations(act, ta, GAT_RING)) as it:
                    for h in range(2):
                        exp_half(act, it, h)

            @block.gpsimd
            def _(pool):
                gather_all(pool)

            @block.vector
            def _(dve):
                attend_free(dve)
                with dve.Fori(0, iterations(dve, ta, GAT_RING)) as it:
                    for h in range(2):
                        attend_half(dve, it, h)

        FT = HID // P
        Y = EXPERTS * D
        scope()
        w1_sb = accf[:, 0:4096].rearrange("p (e c f) -> p e c f", e=EXPERTS, c=2)
        w2_sb = accf[:, 4096:8192].rearrange("p (e k d) -> p e k d", e=EXPERTS, k=FT)
        hh = accf[:, 8192:12288].rearrange("p (e k n) -> p e k n", e=EXPERTS, k=FT)
        b1_sb = sb("b1_sb", [P, EXPERTS, FT])
        b2_sb = te["lists"][:, :].bitcast(F32).rearrange("p (e d) -> p e d", e=EXPERTS)
        y_sb = sb("y_sb", [P, 2, EXPERTS, D])
        hid = [pb(f"hid{i}", [P, 2, 256]) for i in range(4)]
        yp = [pb(f"yp{e_}", [P, 2, D]) for e_ in range(EXPERTS)]
        f_in, hidden_ok, gelu_ok, y_mm, y_ok, y_out, y_in = sems(
            "ffn_loaded", "ffn_hidden", "ffn_gelu", "ffn_product", "ffn_moved", "ffn_stored", "y_loaded")
        in_xt, in_acc = 2 * PADDED // Y, 7
        XTf = flat(XT[:, :, :])
        y_buf = [XTf[:, i * Y:(i + 1) * Y] for i in range(in_xt)] + [accf[:, i * Y:(i + 1) * Y] for i in range(in_acc)]
        PREFETCH = len(y_buf)

        def load_y(sp, w, signal):
            at = y_first if w == 0 else y_rest[(w - 1) // 2, :, (w - 1) % 2 * Y:((w - 1) % 2 + 1) * Y]
            sp.dma_start(y_buf[w % PREFETCH], at).then_inc(signal, 16)

        with nc.Block() as block:
            @block.sync
            def _(sp):
                for x_ in range(EXPERTS):
                    sp.dma_start(w1_sb[:, x_, :, :], w1[x_].rearrange("(c p) f -> p c f", p=P)).then_inc(f_in, 16)
                    sp.dma_start(w2_sb[:, x_, :, :], w2[x_].rearrange("(k p) d -> p k d", p=P)).then_inc(f_in, 16)
                sp.dma_start(b1_sb[:, :, :], b1.rearrange("p (e k) -> p e k", e=EXPERTS)).then_inc(f_in, 16)
                sp.dma_start(b2_sb, b2.unsqueeze(0)).then_inc(f_in, 16)
                sp.wait_ge(y_ok, EXPERTS)
                sp.dma_start(y_first, y_sb[:, 0, :, :].rearrange("p e d -> p (e d)")).then_inc(y_out, 16)
                with sp.Fori(0, PAIRS) as g:
                    sp.wait_ge(y_ok, g * EXPERTS + 2 * EXPERTS)
                    sp.dma_start(y_rest[ds(g, 1), :, :].rearrange("g p n -> p (g n)"),
                                 y_sb[:, :, :, :].rearrange("p v e d -> p (v e d)")).then_inc(y_out, 16)
                sp.wait_ge(y_out, 16 * (PAIRS + 1))
                for w in range(PREFETCH):
                    load_y(sp, w, y_in)
                sp.wait_ge(y_in, 16 * PREFETCH)

            @block.tensor
            def _(pe):
                pe.wait_ge(f_in, 16 * (2 * EXPERTS + 2))

                def hidden(n, e_, first_col, cols):
                    for f in range(FT):
                        bank = e_ % 2 * 2 + f // 2
                        if f % 2 == 0 and not (isinstance(n, int) and n < 2):
                            pe.wait_ge(gelu_ok, (n - 2) * FT + (f + 2))
                        for c in range(2):
                            mm = pe.matmul(hid[bank][:, f % 2, 0:cols], w1_sb[:, e_, c, f * P:(f + 1) * P],
                                           XT[:, c, ds(first_col, cols)], start=(c == 0), stop=(c == 1))
                        mm.then_inc(hidden_ok, 1)

                def output(n, e_, wins):
                    pe.wait_ge(gelu_ok, n * FT + FT)
                    if not (isinstance(n, int) and n < EXPERTS):
                        pe.wait_ge(y_ok, n - (EXPERTS - 1))
                    for v in range(wins):
                        for k in range(FT):
                            pe.matmul(yp[e_][:, v, :], hh[:, e_, k, v * P:(v + 1) * P], w2_sb[:, e_, k, :],
                                      start=(k == 0), stop=False)
                        mm = pe.matmul(yp[e_][:, v, :], ones[0:1, :], b2_sb[:, e_, :], start=False, stop=True)
                    mm.then_inc(y_mm, 1)

                def windows(n0, first_col, wins):
                    hidden(n0, 0, first_col, wins * P)
                    for e_ in range(1, EXPERTS):
                        hidden(n0 + e_, e_, first_col, wins * P)
                        output(n0 + (e_ - 1), e_ - 1, wins)
                    output(n0 + (EXPERTS - 1), EXPERTS - 1, wins)

                windows(0, 0, 1)
                with pe.Fori(0, PAIRS) as g:
                    windows(g * EXPERTS + EXPERTS, g * (2 * P) + P, 2)

            def gelu(act, n, e_, cols):
                if not (isinstance(n, int) and n < EXPERTS):
                    act.wait_ge(y_mm, n - (EXPERTS - 1))
                for f in range(FT):
                    if f % 2 == 0:
                        act.wait_ge(hidden_ok, n * FT + (f + 2))
                    act.activation(hh[:, e_, f, 0:cols], hid[e_ % 2 * 2 + f // 2][:, f % 2, 0:cols], ACT.Gelu,
                                   bias=b1_sb[:, e_, f:f + 1]).then_inc(gelu_ok, 1)

            @block.scalar
            def _(act):
                n = iterations(act, ta, GAT_RING)
                stage_first(act)
                act.wait_ge(f_in, 16 * (2 * EXPERTS + 2))
                for e_ in range(EXPERTS):
                    gelu(act, e_, e_, P)
                with act.Fori(0, PAIRS) as it:
                    for h in range(2):
                        exp_half(act, it, h)
                        for e_ in (2 * h, 2 * h + 1):
                            gelu(act, it * EXPERTS + (EXPERTS + e_), e_, 2 * P)
                with act.Fori(PAIRS, n) as it:
                    for h in range(2):
                        exp_half(act, it, h)

            @block.gpsimd
            def _(pool):
                gather_all(pool)

            @block.vector
            def _(dve):
                n = iterations(dve, ta, GAT_RING)

                def move(k, e_, wins):
                    dve.wait_ge(y_mm, k + 1)
                    dve.tensor_copy(y_sb[:, 0:wins, e_, :], yp[e_][:, 0:wins, :]).then_inc(y_ok, 1)

                attend_free(dve)
                for e_ in range(EXPERTS):
                    move(e_, e_, 1)
                with dve.Fori(0, PAIRS) as it:
                    for h in range(2):
                        attend_half(dve, it, h)
                    dve.wait_ge(y_out, it * 16 + 16)
                    for e_ in range(EXPERTS):
                        move(it * EXPERTS + (EXPERTS + e_), e_, 2)
                with dve.Fori(PAIRS, n) as it:
                    for h in range(2):
                        attend_half(dve, it, h)
        leave()
        more_passes(ta, gat_body, GAT_RING, gat_pass)
        leave()

        scope()
        vec = sb("vec", [P, 3, 16])
        den = sb("den", [P, W, HEADS])
        ag, sqr = (flat(raw[:, :, :])[:, i * W * 16:(i + 1) * W * 16].rearrange("p (w c) -> p w c", c=16) for i in range(2))
        mean, vr, rt = (sb(n, [P, W]) for n in ("g_mean", "g_var", "g_root"))
        sco, rank, ex, gates = (sb(n, [P, W, EXPERTS]) for n in ("sco", "rank", "ex", "gates"))
        less = sb("less", [P, W])
        gate_tmp = accf[:, in_acc * Y:]
        hot, picked = (gate_tmp[:, i * W * W:(i + 1) * W * W].rearrange("p (a b) -> p a b", b=W) for i in range(2))
        v_in, step, a_in, a_out, gates_ok, even_done, odd_done, scaled, added, stored = sems(
            "gat_vec_loaded", "gate_step", "gate_act_in", "gate_act_out", "gates_ready", "even_windows_done",
            "odd_windows_done", "y_scaled", "odd_added", "stored")
        gy = sb("gy", [P, 2, EXPERTS, D])
        xp = [pb(f"xp{i}", [P, D]) for i in range(2)]

        def wait_done(eng, evens, odds):
            for signal, count in ((even_done, evens), (odd_done, odds)):
                if count:
                    eng.wait_ge(signal, count)
        BATCH = 5
        y_more = s_in

        def y_landed(eng, w):
            i = (w - PREFETCH) // BATCH
            x_twice = 2 * (32 if LAST > i * GROUP else 16)
            eng.wait_ge(y_more[i], x_twice + 16 * min(BATCH, W - PREFETCH - i * BATCH))

        with nc.Block() as block:
            @block.sync
            def _(sp):
                for c in range(3):
                    sp.dma_start(vec[:, c, :], gat_vec[c:c + 1, :].to_broadcast([P, 16])).then_inc(v_in, 16)
                outs = 0
                for w in range(W):
                    wait_done(sp, w // 2 + 1, (w + 1) // 2)
                    if w + PREFETCH < W:
                        load_y(sp, w + PREFETCH, y_more[w // BATCH])
                    if w % GROUP == GROUP - 1:
                        g = w // GROUP
                        s, last = slice(g * GROUP, (g + 1) * GROUP), min(LAST, (g + 1) * GROUP)
                        sp.dma_start(out[0:FULL * W, :].rearrange("(p w) d -> p w d", w=W)[:, s, :], X[0:FULL, s, :]).then_inc(stored, 16)
                        outs += 1
                        if last > g * GROUP:
                            sp.dma_start(out[FULL * W + g * GROUP:FULL * W + last, :].unsqueeze(0),
                                         X[FULL:P, g * GROUP:last, :]).then_inc(stored, 16)
                            outs += 1
                sp.wait_ge(stored, 16 * outs)

            @block.scalar
            def _(act):
                act.wait_ge(a_in, 1)
                act.activation(rt[:, :], vr[:, :], ACT.Sqrt).then_inc(a_out, 1)
                act.wait_ge(a_in, 2)
                act.activation(ex[:, :, :], sco[:, :, :], ACT.Exp).then_inc(a_out, 1)
                act.wait_ge(gates_ok, 1)

                def take(k):
                    act.wait_ge(added, k + 1)
                    act.activation(X[:, 2 * k + 1, :], xp[k % 2][:, :], ACT.Copy).then_inc(odd_done, 1)

                for k in range(W // 2):
                    w = 2 * k + 1
                    if w >= PREFETCH:
                        y_landed(act, w)
                    if k >= 2:
                        act.wait_ge(added, k - 1)
                    for e_ in range(EXPERTS):
                        act.activation(gy[:, k % 2, e_, :], y_buf[w % PREFETCH][:, e_ * D:(e_ + 1) * D], ACT.Copy,
                                       scale=gates[:, w, e_:e_ + 1]).then_inc(scaled, 1)
                    if k:
                        take(k - 1)
                take(W // 2 - 1)

            @block.tensor
            def _(pe):
                for k in range(W // 2):
                    if k >= 2:
                        pe.wait_ge(odd_done, k - 1)
                    pe.matmul(xp[k % 2][:, :], ident, X[:, 2 * k + 1, :], start=True, stop=False)
                    for e_ in range(EXPERTS):
                        pe.wait_ge(scaled, k * EXPERTS + e_ + 1)
                        mm = pe.matmul(xp[k % 2][:, :], ident, gy[:, k % 2, e_, :], start=False, stop=e_ == EXPERTS - 1)
                    mm.then_inc(added, 1)

            @block.vector
            def _(dve):
                link = link_on(dve, step)
                dve.wait_ge(v_in, 48)
                sv = state[:, 0:W, :].rearrange("p w (h e) -> p w h e", h=HEADS)
                def wide(a):
                    return a[:, :].unsqueeze(2).to_broadcast([P, W, 16])
                def row(c):
                    return vec[:, c, :].unsqueeze(1).to_broadcast([P, W, 16])
                a4 = ag[:, :, :].rearrange("p w (h e) -> p w h e", h=HEADS)
                link(dve.tensor_scalar(den[:, :, :], sv[:, :, :, EXPERTS], 1e-16, None, ALU.add))
                link(dve.reciprocal(den[:, :, :], den[:, :, :]))
                link(dve.tensor_tensor(a4, sv[:, :, :, 0:EXPERTS], den[:, :, :].unsqueeze(3).to_broadcast([P, W, HEADS, EXPERTS]), ALU.mult))
                link(dve.tensor_tensor(ag[:, :, :], ag[:, :, :], row(0), ALU.add))
                link(dve.tensor_reduce(mean[:, :], ag[:, :, :], AX.X, ALU.add))
                link(dve.tensor_scalar(mean[:, :], mean[:, :], 1.0 / 16, None, ALU.mult))
                link(dve.tensor_tensor(ag[:, :, :], ag[:, :, :], wide(mean), ALU.subtract))
                link(dve.tensor_tensor(sqr[:, :, :], ag[:, :, :], ag[:, :, :], ALU.mult))
                link(dve.tensor_reduce(vr[:, :], sqr[:, :, :], AX.X, ALU.add))
                link(dve.tensor_scalar(vr[:, :], vr[:, :], 1.0 / 16, EPS, ALU.mult, ALU.add))
                dve.sem_inc(a_in, 1)
                link(dve.tensor_tensor(hot, iota[:, 0:W].unsqueeze(2).to_broadcast([P, W, W]),
                                       ta["kw"][:, 0:W].unsqueeze(1).to_broadcast([P, W, W]), ALU.is_equal))
                dve.wait_ge(a_out, 1)
                link(dve.reciprocal(rt[:, :], rt[:, :]))
                link(dve.tensor_tensor(ag[:, :, :], ag[:, :, :], wide(rt), ALU.mult))
                link(dve.tensor_tensor(ag[:, :, :], ag[:, :, :], row(1), ALU.mult))
                link(dve.tensor_tensor(ag[:, :, :], ag[:, :, :], row(2), ALU.add))
                link(dve.tensor_reduce(sco[:, :, :], ag[:, :, :].rearrange("p w (h e) -> p w e h", h=HEADS), AX.X, ALU.add))
                link(dve.tensor_scalar(sco[:, :, :], sco[:, :, :], 1.0 / HEADS, None, ALU.mult), dve.memset(rank[:, :, :], 0.0))
                for e_ in range(EXPERTS):
                    for f in range(e_):
                        link(dve.tensor_tensor(less[:, :], sco[:, :, f], sco[:, :, e_], ALU.is_ge))
                        link(dve.tensor_tensor(rank[:, :, e_], rank[:, :, e_], less[:, :], ALU.add))
                        link(dve.tensor_tensor(less[:, :], sco[:, :, f], sco[:, :, e_], ALU.is_lt))
                        link(dve.tensor_tensor(rank[:, :, f], rank[:, :, f], less[:, :], ALU.add))
                link(dve.tensor_reduce(mean[:, :], sco[:, :, :], AX.X, ALU.max))
                link(dve.tensor_tensor(sco[:, :, :], sco[:, :, :], mean[:, :].unsqueeze(2).to_broadcast([P, W, EXPERTS]), ALU.subtract))
                dve.sem_inc(a_in, 1)
                dve.wait_ge(a_out, 2)
                link(dve.scalar_tensor_tensor(ex[:, :, :], rank[:, :, :], float(TOP), ex[:, :, :], ALU.is_lt, ALU.mult))
                link(dve.tensor_reduce(mean[:, :], ex[:, :, :], AX.X, ALU.add))
                link(dve.reciprocal(mean[:, :], mean[:, :]))
                link(dve.tensor_tensor(ex[:, :, :], ex[:, :, :], mean[:, :].unsqueeze(2).to_broadcast([P, W, EXPERTS]), ALU.mult))
                for e_ in range(EXPERTS):
                    link(dve.tensor_tensor(picked, hot, ex[:, :, e_].unsqueeze(1).to_broadcast([P, W, W]), ALU.mult))
                    link(dve.tensor_reduce(gates[:, :, e_], picked, AX.X, ALU.add))
                dve.sem_inc(gates_ok, 1)
                for w in range(0, W, 4):
                    pair = [v for v in (w, w + 2) if v < W]
                    for v in pair:
                        if v >= PREFETCH:
                            y_landed(dve, v)
                    for e_ in range(EXPERTS):
                        link(*[dve.scalar_tensor_tensor(X[:, v, :], y_buf[v % PREFETCH][:, e_ * D:(e_ + 1) * D],
                                                        gates[:, v, e_:e_ + 1], X[:, v, :], ALU.mult, ALU.add) for v in pair])
                    dve.sem_inc(even_done, len(pair))
        leave()
        leave()


def constants():
    import numpy as np
    c = np.zeros((P, C_END), np.float32)
    p = np.arange(P)
    c[:, C_ID:C_ID + P] = np.eye(P)

    def direction(k):
        return np.where((p >> (k - 10)) & 1, -1.0, 1.0)

    c[:, C_SIGN] = direction(10)
    for k in range(11, 18):
        c[:, C_SIGN + k - 10] = direction(k - 1) * direction(k)
    for bit in (5, 6):
        c[:, C_SIGN + bit + 3] = np.where((p >> bit) & 1, -1.0, 1.0)
    c[:, C_NODE:C_NODE + SLOTS] = p[:, None] * W + np.arange(SLOTS)
    c[:, C_IOTA:C_IOTA + P] = np.arange(P)
    c[:, C_Q:C_END] = np.arange(CHUNKS // P) * P + p[:, None]
    return c


def lay_out(i):
    import numpy as np
    a = {k: np.ascontiguousarray(v) for k, v in i.items()}
    cat, tile = np.concatenate, np.tile
    m = "L0_mix_"
    f = "L0_ffn_"
    t = lambda v: np.ascontiguousarray(v.T)
    return {
        "x": a["x"], "src": a["src"], "dst": a["dst"], "gat_edges": a[f + "edge_index"],
        "gnn_w": a["L0_gnn_W"], "wq": a[m + "wq"], "wk_t": t(a[m + "wk"]), "wv_t": t(a[m + "wv"]),
        "wo_t": t(a[m + "wo"]), "bo": a[m + "bo"],
        "lnkv": np.stack([cat([tile(a[m + "ln_k_g"], 4), tile(a[m + "ln_v_g"], 4)]),
                          cat([tile(a[m + "ln_k_b"], 4), tile(a[m + "ln_v_b"], 4)])]),
        "gat_w": a[f + "W_gat"],
        "att": np.stack([a[f + "att_src"].reshape(-1), a[f + "att_dst"].reshape(-1)]),
        "gat_vec": np.stack([a[f + "b_gat"], a[f + "ln_gamma"], a[f + "ln_beta"]]),
        "w1": a[f + "W1"], "b1": np.ascontiguousarray(a[f + "b1"].reshape(EXPERTS * HID // P, P).T),
        "w2": a[f + "W2"], "b2": a[f + "b2"], "consts": constants(),
    }


def kernel(**inputs):
    import numpy as np
    import concourse.bacc as bacc
    from concourse.bass_utils import run_bass_kernel_spmd as run

    nc = bacc.Bacc("TRN2", target_bir_lowering=False, num_devices=1)
    arrays, args = {}, []
    for name, a in lay_out(inputs).items():
        arrays["in_" + name] = a
        args.append(nc.dram_tensor("in_" + name, a.shape, mybir.dt.from_np(a.dtype), kind="ExternalInput").ap())
    o = nc.dram_tensor("out", (NODES, D), F32, kind="ExternalOutput").ap()
    build(nc, *args, o)
    r = run(nc, [arrays], core_ids=[0])
    return r.results[0]["out"]
```
